# Optimizing a Trainium2 kernel written in Bass

```python
import numpy as np
import jax
import jax.numpy as jnp

def _softmax(x, axis=-1):
    return jax.nn.softmax(x, axis=axis)

def _gelu(x):
    return jax.nn.gelu(x, approximate=True)

def _silu(x):
    return jax.nn.silu(x)

def _sigmoid(x):
    return jax.nn.sigmoid(x)

def _layernorm(x, axis=-1, eps=1e-05):
    m = jnp.mean(x, axis=axis, keepdims=True)
    v = jnp.var(x, axis=axis, keepdims=True)
    return (x - m) / jnp.sqrt(v + eps)

def _scatter_add(tgt, idx, src, axis=0):
    return tgt.at[idx].add(src)

def _segment_sum(src, seg, n):
    return jax.ops.segment_sum(src, seg, n)
kernel_name = 'mk_cond_seq_d1_seqx_r2_5cddd0'

def setup_inputs(seed: int=0):
    np.random.seed(seed)
    _w = jnp.asarray

    def _rec_inputs():
        import jax
        import jax.numpy as jnp
        _rk = jax.random.key(seed)
        x = 7.22e-05 + 1 * jax.random.normal(jax.random.fold_in(_rk, 1), (64, 128, 512), jnp.float32)
        _lenS = 128 - jax.random.randint(jax.random.fold_in(_rk, 7), (64,), 0, max(1, 128 // 4) + 1, jnp.int32)
        _lenS2 = 128 - jax.random.randint(jax.random.fold_in(_rk, 8), (64,), 0, max(1, 128 // 4) + 1, jnp.int32)
        cond_1024 = 0.0061147 + 1.02565 * jax.random.normal(jax.random.fold_in(_rk, 11), (64, 512), jnp.float32)
        return (x, cond_1024)
    x, cond_1024 = _rec_inputs()

    def _L0_cond_setup():
        import jax, jax.numpy as jnp
        import numpy as np
        DIM = 512
        MLP_RATIO = 4
        EPS = 1e-06

        def rmsnorm(x, w):
            return x * jax.lax.rsqrt(jnp.mean(x * x, axis=-1, keepdims=True) + EPS) * w

        def film(x, cond, w, b):
            ss = cond @ w + b
            scale, shift = jnp.split(ss, 2, axis=-1)
            return x * (1.0 + scale[:, None, :]) + shift[:, None, :]
        key = jax.random.key(seed)
        ks = jax.random.split(key, 16)
        B, N, D = (4, 1024, DIM)
        H = D * MLP_RATIO
        s = lambda fan_in: 1.0 / np.sqrt(fan_in)
        return {'x': jax.random.normal(ks[0], (B, N, D), jnp.float32), 'cond': jax.random.normal(ks[1], (B, D), jnp.float32), 'norm1_w': jnp.ones((D,), jnp.float32), 'film1_w': jax.random.normal(ks[2], (D, 2 * D), jnp.float32) * s(D), 'film1_b': jnp.zeros((2 * D,), jnp.float32), 'q_w': jax.random.normal(ks[3], (D, D), jnp.float32) * s(D), 'q_b': jnp.zeros((D,), jnp.float32), 'k_w': jax.random.normal(ks[4], (D, D), jnp.float32) * s(D), 'k_b': jnp.zeros((D,), jnp.float32), 'v_w': jax.random.normal(ks[5], (D, D), jnp.float32) * s(D), 'v_b': jnp.zeros((D,), jnp.float32), 'proj_w': jax.random.normal(ks[6], (D, D), jnp.float32) * s(D), 'proj_b': jnp.zeros((D,), jnp.float32), 'norm2_w': jnp.ones((D,), jnp.float32), 'film2_w': jax.random.normal(ks[7], (D, 2 * D), jnp.float32) * s(D), 'film2_b': jnp.zeros((2 * D,), jnp.float32), 'mlp_w1': jax.random.normal(ks[8], (D, H), jnp.float32) * s(D), 'mlp_b1': jnp.zeros((H,), jnp.float32), 'mlp_w2': jax.random.normal(ks[9], (H, D), jnp.float32) * s(H), 'mlp_b2': jnp.zeros((D,), jnp.float32)}
    _L0_cond_all = _L0_cond_setup()
    _L0_cond_in = {k: v for k, v in _L0_cond_all.items() if k in ('norm1_w', 'film1_w', 'film1_b', 'q_w', 'q_b', 'k_w', 'k_b', 'v_w', 'v_b', 'proj_w', 'proj_b', 'norm2_w', 'film2_w', 'film2_b', 'mlp_w1', 'mlp_b1', 'mlp_w2', 'mlp_b2')}
    del _L0_cond_all
    return {'x': x, 'cond_1024': cond_1024, 'L0_cond_norm1_w': _L0_cond_in['norm1_w'], 'L0_cond_film1_w': _L0_cond_in['film1_w'], 'L0_cond_film1_b': _L0_cond_in['film1_b'], 'L0_cond_q_w': _L0_cond_in['q_w'], 'L0_cond_q_b': _L0_cond_in['q_b'], 'L0_cond_k_w': _L0_cond_in['k_w'], 'L0_cond_k_b': _L0_cond_in['k_b'], 'L0_cond_v_w': _L0_cond_in['v_w'], 'L0_cond_v_b': _L0_cond_in['v_b'], 'L0_cond_proj_w': _L0_cond_in['proj_w'], 'L0_cond_proj_b': _L0_cond_in['proj_b'], 'L0_cond_norm2_w': _L0_cond_in['norm2_w'], 'L0_cond_film2_w': _L0_cond_in['film2_w'], 'L0_cond_film2_b': _L0_cond_in['film2_b'], 'L0_cond_mlp_w1': _L0_cond_in['mlp_w1'], 'L0_cond_mlp_b1': _L0_cond_in['mlp_b1'], 'L0_cond_mlp_w2': _L0_cond_in['mlp_w2'], 'L0_cond_mlp_b2': _L0_cond_in['mlp_b2']}

def reference(x, cond_1024, L0_cond_norm1_w, L0_cond_film1_w, L0_cond_film1_b, L0_cond_q_w, L0_cond_q_b, L0_cond_k_w, L0_cond_k_b, L0_cond_v_w, L0_cond_v_b, L0_cond_proj_w, L0_cond_proj_b, L0_cond_norm2_w, L0_cond_film2_w, L0_cond_film2_b, L0_cond_mlp_w1, L0_cond_mlp_b1, L0_cond_mlp_w2, L0_cond_mlp_b2):
    import jax
    import jax.numpy as jnp

    def _L0_cond_ref(x, cond, norm1_w, film1_w, film1_b, q_w, q_b, k_w, k_b, v_w, v_b, proj_w, proj_b, norm2_w, film2_w, film2_b, mlp_w1, mlp_b1, mlp_w2, mlp_b2):
        import jax, jax.numpy as jnp
        import numpy as np
        DIM = 512
        MLP_RATIO = 4
        EPS = 1e-06

        def rmsnorm(x, w):
            return x * jax.lax.rsqrt(jnp.mean(x * x, axis=-1, keepdims=True) + EPS) * w

        def film(x, cond, w, b):
            ss = cond @ w + b
            scale, shift = jnp.split(ss, 2, axis=-1)
            return x * (1.0 + scale[:, None, :]) + shift[:, None, :]
        B, N, D = x.shape
        x_in = x
        h = film(rmsnorm(x, norm1_w), cond, film1_w, film1_b)
        Q = h @ q_w + q_b
        K = h @ k_w + k_b
        V = h @ v_w + v_b
        scores = jnp.einsum('bnd,bmd->bnm', Q, K) * D ** (-0.5)
        attn = jax.nn.softmax(scores, axis=-1)
        out = jnp.einsum('bnm,bmd->bnd', attn, V)
        x = x_in + (out @ proj_w + proj_b)
        x_in = x
        h = film(rmsnorm(x, norm2_w), cond, film2_w, film2_b)
        h = jax.nn.gelu(h @ mlp_w1 + mlp_b1, approximate=False) @ mlp_w2 + mlp_b2
        return x_in + h
    x = _L0_cond_ref(x, cond_1024, L0_cond_norm1_w, L0_cond_film1_w, L0_cond_film1_b, L0_cond_q_w, L0_cond_q_b, L0_cond_k_w, L0_cond_k_b, L0_cond_v_w, L0_cond_v_b, L0_cond_proj_w, L0_cond_proj_b, L0_cond_norm2_w, L0_cond_film2_w, L0_cond_film2_b, L0_cond_mlp_w1, L0_cond_mlp_b1, L0_cond_mlp_w2, L0_cond_mlp_b2)
    return x

_drawn_inputs = setup_inputs


def setup_inputs(seed=0):
    import zlib

    import numpy as np

    out = dict(_drawn_inputs(seed))
    spreads = {'L0_cond_norm1_w': (1.0, 0.2),
     'L0_cond_film1_b': (0.0, 0.1),
     'L0_cond_q_b': (0.0, 0.1),
     'L0_cond_k_b': (0.0, 0.1),
     'L0_cond_v_b': (0.0, 0.1),
     'L0_cond_proj_b': (0.0, 0.1),
     'L0_cond_norm2_w': (1.0, 0.2),
     'L0_cond_film2_b': (0.0, 0.1),
     'L0_cond_mlp_b1': (0.0, 0.1),
     'L0_cond_mlp_b2': (0.0, 0.1)}
    factors = {}
    for name, (base, spread) in spreads.items():
        noise = np.random.default_rng([zlib.crc32(name.encode()), seed]).standard_normal(out[name].shape)
        drawn = base * np.exp(spread * noise) if base else spread * noise
        out[name] = jnp.asarray(drawn.astype(out[name].dtype))
    for name, factor in factors.items():
        out[name] = (out[name] * factor).astype(out[name].dtype)
    return out
```

```python
from contextlib import ExitStack

import concourse.bass as bass
from concourse import mybir

F32 = mybir.dt.float32
F32R = mybir.dt.float32r
ACT = mybir.ActivationFunctionType
ALU = mybir.AluOpType
AX_X = mybir.AxisListType.X

P = 128
EPS = 1e-6


class Shapes:

    def __init__(self, x, w1):
        self.B, self.N, self.D = x.shape
        self.H = w1.shape[1]
        assert self.N == P and self.D % P == 0
        self.KD = self.D // P
        self.KH = self.H // P
        self.GB = 4
        self.TOK = self.GB * P
        self.GROUPS = self.B // self.GB
        self.PAIRS = self.GROUPS // 2


def column_map(s):
    at, out = 0, {}
    for name, n in (("n1", s.KD), ("f1b", 2 * s.KD), ("bq", s.KD), ("bk", s.KD), ("bv", s.KD),
                    ("n2", s.KD), ("f2b", 2 * s.KD), ("b1", s.KH)):
        out[name] = (at, at + n)
        at += n
    return out, at


def split3(hi_a, lo_a, hi_b, lo_b):
    return ((hi_a, hi_b), (hi_a, lo_b), (lo_a, hi_b))


def wait_used(engine, sem, uses):
    if not isinstance(uses, int) or uses > 0:
        engine.wait_ge(sem, uses)


def pairs(engine, s, body, first=None):
    if first:
        first()
    for p in range(2):
        body(p, p, 0, True)
    with engine.Fori(1, s.PAIRS - 1) as i:
        for p in range(2):
            body(2 * i + p, p, i, True)
    i = s.PAIRS - 1
    for p in range(2):
        body(2 * i + p, p, i, p == 0)


def setup_stage(nc, s, dram, keep, cmap):
    KD, D = s.KD, s.D
    with ExitStack() as ctx:
        def sb(name, shape, dt=F32):
            return ctx.enter_context(nc.sbuf_tensor(name, shape, dt))

        def sem(name):
            return ctx.enter_context(nc.semaphore(name))

        wqT, wkT, wvT, wp = (sb(n, [P, KD, D]) for n in ("wqT", "wkT", "wvT", "wp"))
        f1w, f2w = (sb(n, [P, KD, 2 * D]) for n in ("f1w", "f2w"))
        condT = sb("condT", [P, KD, s.B])
        bv_wide = sb("bv_wide", [P, KD, P])
        bp_wide = sb("bp_wide", [P, D])
        scale_bias = sb("scale_bias", [P, 2, KD])
        prod = ctx.enter_context(nc.psum_tensor("prod", [P, 4, D], F32))
        vec = ctx.enter_context(nc.psum_tensor("vec", [P, D], F32))
        film = ctx.enter_context(nc.psum_tensor("film", [P, 2, 2 * KD, s.B], F32))

        loads = ("cols", "condT", "wqT", "wkT", "wvT", "wp", "f1w", "f2w", "bp", "b2")
        loaded = {n: sem("loaded_" + n) for n in loads}
        ident_zero, ident_done, ones_done = sem("ident_zero"), sem("ident_done"), sem("ones_done")
        bv_ready = sem("bv_ready")
        prod_full = [sem(f"prod_full{r}") for r in range(4)]
        prod_hi = [sem(f"prod_hi{r}") for r in range(4)]
        prod_lo = [sem(f"prod_lo{r}") for r in range(4)]
        vec_full, row_full, vec_read, row_read = sem("vec_full"), sem("row_full"), sem("vec_read"), sem("row_read")
        film_full = [sem("film_full0"), sem("film_full1")]
        one_plus, bias_products, coef_done = sem("one_plus"), sem("bias_products"), sem("coef_done")

        def col(name):
            a, b = cmap[name]
            return keep["cols"][:, a:b]

        block = ctx.enter_context(nc.Block())

        @block.sync
        def _(sp):
            def chunked(name):
                return dram[name].rearrange("(k p) n -> p k n", p=P)
            sp.dma_start(wqT[:], chunked("wqT")).then_inc(loaded["wqT"], 16)
            sp.dma_start(wkT[:], chunked("wkT")).then_inc(loaded["wkT"], 16)
            sp.dma_start(keep["cols"][:], dram["cols"]).then_inc(loaded["cols"], 16)
            sp.dma_start(wvT[:], chunked("wvT")).then_inc(loaded["wvT"], 16)
            sp.dma_start(wp[:], chunked("wp")).then_inc(loaded["wp"], 16)
            sp.dma_start(condT[:], chunked("condT")).then_inc(loaded["condT"], 16)
            sp.dma_start(f1w[:], chunked("f1w")).then_inc(loaded["f1w"], 16)
            sp.dma_start(bp_wide[:], dram["rows"][0:1, :].broadcast_to([P, D])).then_inc(loaded["bp"], 16)
            sp.dma_start(keep["b2_wide"][:], dram["rows"][1:2, :].broadcast_to([P, D])).then_inc(loaded["b2"], 16)
            sp.dma_start(f2w[:], chunked("f2w")).then_inc(loaded["f2w"], 16)

        @block.gpsimd
        def _(pool):
            nc.gpsimd.memset(keep["ident"][:], 0.0).then_inc(ident_zero, 1)
            pool.wait_ge(ident_zero, 1)
            nc.gpsimd.affine_select(out=keep["ident"][:], in_=keep["ident"][:], compare_op=ALU.not_equal, fill=1.0,
                                    base=0, pattern=[[-1, P]], channel_multiplier=1).then_inc(ident_done, 1)
            nc.gpsimd.memset(keep["ones"][:], 1.0).then_inc(ones_done, 1)
            nc.gpsimd.memset(keep["minus_half"][:], -0.5).then_inc(ones_done, 1)
            nc.gpsimd.memset(keep["eps_sum"][:], EPS * D).then_inc(ones_done, 1)

        @block.tensor
        def _(pe):
            pe.wait_ge(loaded["wqT"], 16)
            pe.wait_ge(loaded["wkT"], 16)
            for m in range(KD):
                for k in range(KD):
                    mm = pe.matmul(prod[:, m, :], wqT[:, k, m * P:(m + 1) * P], wkT[:, k, :],
                                   start=k == 0, stop=k == KD - 1)
                mm.then_inc(prod_full[m], 1)
            pe.wait_ge(loaded["cols"], 16)
            for v, (w, b) in enumerate(((wkT, "bq"), (wqT, "bk"))):
                for m in range(KD):
                    for k in range(KD):
                        mm = pe.matmul(vec[:, v * KD + m:v * KD + m + 1], w[:, k, m * P:(m + 1) * P],
                                       col(b)[:, k:k + 1], start=k == 0, stop=k == KD - 1)
            mm.then_inc(vec_full, 1)
            pe.wait_ge(loaded["wvT"], 16)
            pe.wait_ge(loaded["wp"], 16)
            for m in range(KD):
                pe.wait_ge(prod_lo[m], 1)
                for k in range(KD):
                    mm = pe.matmul(prod[:, m, :], wvT[:, k, m * P:(m + 1) * P], wp[:, k, :],
                                   start=k == 0, stop=k == KD - 1)
                mm.then_inc(prod_full[m], 1)
            pe.wait_ge(bv_ready, 1)
            pe.wait_ge(vec_read, 2)
            for k in range(KD):
                mm = pe.matmul(vec[:], bv_wide[:, k, :], wp[:, k, :], start=k == 0, stop=k == KD - 1)
            mm.then_inc(row_full, 1)
            pe.wait_ge(loaded["condT"], 16)
            for f, (w, name) in enumerate(((f1w, "f1w"), (f2w, "f2w"))):
                pe.wait_ge(loaded[name], 16)
                for j in range(2 * KD):
                    for k in range(KD):
                        mm = pe.matmul(film[:, f, j, :], w[:, k, j * P:(j + 1) * P], condT[:, k, :],
                                       start=k == 0, stop=k == KD - 1)
                mm.then_inc(film_full[f], 1)

        @block.scalar
        def _(act):
            for w, hi in enumerate((keep["qk_hi"], keep["vp_hi"])):
                for m in range(KD):
                    act.wait_ge(prod_full[m], w + 1)
                    nc.scalar.copy(hi[:, m, :], prod[:, m, :]).then_inc(prod_hi[m], 1)

        @block.vector
        def _(dve):
            def low_parts(w, hi, lo):
                for m in range(KD):
                    dve.wait_ge(prod_hi[m], w + 1)
                    dve.tensor_tensor(lo[:, m, :], prod[:, m, :], hi[:, m, :].bitcast(F32),
                                      ALU.subtract).then_inc(prod_lo[m], 1)

            low_parts(0, keep["qk_hi"], keep["qk_lo"])
            dve.wait_ge(loaded["cols"], 16)
            for k in range(KD):
                last = dve.tensor_copy(bv_wide[:, k, :], col("bv")[:, k:k + 1].broadcast_to([P, P]))
            last.then_inc(bv_ready, 1)
            dve.wait_ge(vec_full, 1)
            dve.tensor_copy(keep["wk_bq"][:], vec[:, 0:KD]).then_inc(vec_read, 1)
            dve.tensor_copy(keep["wq_bk"][:], vec[:, KD:2 * KD]).then_inc(vec_read, 1)
            dve.tensor_tensor_reduce(keep["bq_bk_terms"][:], col("bq"), col("bk"), 1.0, 0.0, ALU.mult, ALU.add,
                                     keep["bq_bk"][:]).then_inc(bias_products, 1)
            for f, (b, n) in enumerate((("f1b", "n1"), ("f2b", "n2"))):
                dve.tensor_scalar(scale_bias[:, f, :], col(b)[:, 0:KD], 1.0, None, ALU.add).then_inc(one_plus, 1)
            low_parts(1, keep["vp_hi"], keep["vp_lo"])
            dve.wait_ge(row_full, 1)
            dve.wait_ge(loaded["bp"], 16)
            dve.tensor_tensor(keep["attn_bias"][:], vec[:], bp_wide[:], ALU.add).then_inc(row_read, 1)
            dve.wait_ge(one_plus, 2)
            for f, (b, n) in enumerate((("f1b", "n1"), ("f2b", "n2"))):
                dve.wait_ge(film_full[f], 1)
                for k in range(KD):
                    dve.tensor_scalar(keep["film"][f][:, k, :], film[:, f, k, :], scale_bias[:, f, k:k + 1],
                                      col(n)[:, k:k + 1], ALU.add, ALU.mult).then_inc(coef_done, 1)
                    dve.tensor_scalar(keep["film"][f][:, KD + k, :], film[:, f, KD + k, :],
                                      col(b)[:, KD + k:KD + k + 1], None, ALU.add).then_inc(coef_done, 1)


def attention_stage(nc, s, x_dram, x2_dram, keep):
    KD, GB, TOK, D = s.KD, s.GB, s.TOK, s.D
    SCALE = float(D) ** -0.5
    with ExitStack() as ctx:
        def sb(name, shape, dt=F32):
            return ctx.enter_context(nc.sbuf_tensor(name, shape, dt))

        def ps(name, shape):
            return ctx.enter_context(nc.psum_tensor(name, shape, F32))

        def sem(name):
            return ctx.enter_context(nc.semaphore("a_" + name))

        def sems(name, n):
            return [sem(f"{name}{i}") for i in range(n)]

        x_in = [sb(f"ax_in{p}", [P, GB, D]) for p in range(2)]
        x_norm = [sb(f"ax_norm{r}", [P, D]) for r in range(2)]
        square = sb("a_square", [P, D])
        sumsq, rstd = sb("a_sumsq", [P, GB]), sb("a_rstd", [P, GB])
        coef = sb("a_coef", [P, 2 * KD, GB])
        h = [sb(f"ah{p}", [P, KD, TOK]) for p in range(2)]
        h_hi = [sb(f"ah_hi{p}", [P, KD, TOK], F32R) for p in range(2)]
        h_lo = [sb(f"ah_lo{p}", [P, KD, TOK], F32R) for p in range(2)]
        key_bias = sb("a_key_bias", [P, TOK])
        g = sb("a_g", [P, KD, TOK])
        v_hi, v_lo = sb("av_hi", [P, GB, D], F32R), sb("av_lo", [P, GB, D], F32R)
        probs = sb("a_probs", [P, GB, P])
        top, bias, den, rden = (sb("a_" + n, [P, GB]) for n in ("top", "exp_bias", "den", "rden"))
        pT_hi, pT_lo = sb("apT_hi", [P, TOK], F32R), sb("apT_lo", [P, TOK], F32R)
        ring = [ps(f"a_ring{r}", [P, D]) for r in range(4)]
        turn = [ps(f"a_turn{r}", [P, KD, P]) for r in range(2)]
        score = ps("a_score", [P, GB, P])
        pT = ps("a_pT", [P, TOK])

        x_loaded, x2_stored = sems("x_loaded", 2), sems("x2_stored", 2)
        summed, eps_added, rstd_done = sem("summed"), sem("eps_added"), sem("rstd_done")
        normed, biased = sem("normed"), sem("biased")
        turn_full, turn_read = sems("turn_full", 2), sems("turn_read", 2)
        coef_ready, h_hi_done, h_lo_done, key_bias_done = (
            sem(n) for n in ("coef_ready", "h_hi_done", "h_lo_done", "key_bias_done"))
        ring_full, ring_read = sems("ring_full", 4), sems("ring_read", 4)
        v_hi_done, scored, top_done, bias_done, exp_done = (
            sem(n) for n in ("v_hi_done", "scored", "top_done", "bias_done", "exp_done"))
        pT_full, pT_hi_done, pT_read, rden_done = (
            sem(n) for n in ("pT_full", "pT_hi_done", "pT_read", "rden_done"))

        x_groups = x_dram.rearrange("(g b) t d -> g t b d", b=GB)
        x2_groups = x2_dram.rearrange("(g b) t d -> g t b d", b=GB)
        block = ctx.enter_context(nc.Block())

        @block.sync
        def _(sp):
            def load(n, p):
                sp.dma_start(x_in[p][:], x_groups[n]).then_inc(x_loaded[p], 16)

            def group(n, p, i, more):
                for b in range(GB):
                    sp.wait_ge(ring_read[b], 3 * n + 3)
                sp.dma_start(x2_groups[n], x_in[p][:]).then_inc(x2_stored[p], 16)
                sp.wait_ge(x2_stored[p], 16 * i + 16)
                if not isinstance(i, int) or i < s.PAIRS - 1:
                    load(n + 2, p)

            load(0, 0)
            load(1, 1)
            pairs(sp, s, group)

        @block.gpsimd
        def _(pool):
            def norm(n, p):
                pool.wait_ge(summed, GB * n + GB)
                nc.gpsimd.tensor_tensor(rstd[:], sumsq[:], keep["eps_sum"][:].broadcast_to([P, GB]),
                                        ALU.add).then_inc(eps_added, 1)
                pool.wait_ge(eps_added, n + 1)
                nc.gpsimd.tensor_tensor(rstd[:], rstd[:], keep["minus_half"][:].broadcast_to([P, GB]),
                                        ALU.pow).then_inc(rstd_done, 1)
                pool.wait_ge(normed, GB * n + GB)
                for b in range(GB):
                    last = nc.gpsimd.tensor_tensor(x_in[p][:, b, :], x_in[p][:, b, :], keep["attn_bias"][:], ALU.add)
                last.then_inc(biased, 1)

            def group(n, p, i, more):
                if more:
                    norm(n + 1, 1 - p)

            pairs(pool, s, group, lambda: norm(0, 0))

        def transpose_x(pe, n, b):
            r = b % 2
            pe.wait_ge(normed, GB * n + b + 1)
            wait_used(pe, turn_read[r], 2 * n + b // 2)
            for k in range(KD):
                mm = pe.transpose(turn[r][:, k, :], x_norm[r][:, k * P:(k + 1) * P], keep["ident"][:])
            mm.then_inc(turn_full[r], 1)

        @block.tensor
        def _(pe):
            def g_product(n, p):
                pe.wait_ge(h_hi_done, GB * n + GB)
                pe.wait_ge(h_lo_done, GB * n + GB)
                for j in range(KD):
                    wait_used(pe, ring_read[j], 3 * n)
                    steps = [t for k in range(KD) for t in split3(
                        keep["qk_hi"][:, k, j * P:(j + 1) * P], keep["qk_lo"][:, k, j * P:(j + 1) * P],
                        h_hi[p][:, k, :], h_lo[p][:, k, :])]
                    for t, (a, m) in enumerate(steps):
                        mm = pe.matmul(ring[j][:], a, m, start=t == 0, stop=t == len(steps) - 1)
                    mm.then_inc(ring_full[j], 1)

            def v_product(n, p, b):
                pe.wait_ge(ring_read[b], 3 * n + 1)
                tok = slice(b * P, (b + 1) * P)
                steps = [t for k in range(KD) for t in split3(
                    h_hi[p][:, k, tok], h_lo[p][:, k, tok], keep["vp_hi"][:, k, :], keep["vp_lo"][:, k, :])]
                for t, (a, m) in enumerate(steps):
                    mm = pe.matmul(ring[b][:], a, m, start=t == 0, stop=t == len(steps) - 1)
                mm.then_inc(ring_full[b], 1)

            def scores(n, p):
                for j in range(KD):
                    pe.wait_ge(ring_read[j], 3 * n + 1)
                pe.wait_ge(key_bias_done, KD * n + KD)
                wait_used(pe, exp_done, GB * n)
                for b in range(GB):
                    tok = slice(b * P, (b + 1) * P)
                    for k in range(KD):
                        pe.matmul(score[:, b, :], g[:, k, tok], h[p][:, k, tok], start=k == 0, stop=False)
                    mm = pe.matmul(score[:, b, :], key_bias[:, tok], keep["ones"][:], start=False, stop=True)
                mm.then_inc(scored, 1)

            def transpose_probs(n):
                pe.wait_ge(exp_done, GB * n + GB)
                wait_used(pe, pT_read, n)
                for b in range(GB):
                    mm = pe.transpose(pT[:, b * P:(b + 1) * P], probs[:, b, :], keep["ident"][:])
                mm.then_inc(pT_full, 1)

            def output(n, b):
                pe.wait_ge(pT_read, n + 1)
                pe.wait_ge(ring_read[b], 3 * n + 2)
                tok = slice(b * P, (b + 1) * P)
                for t, (a, m) in enumerate(split3(pT_hi[:, tok], pT_lo[:, tok], v_hi[:, b, :], v_lo[:, b, :])):
                    mm = pe.matmul(ring[b][:], a, m, start=t == 0, stop=t == 2)
                mm.then_inc(ring_full[b], 1)

            def first():
                for b in range(GB):
                    transpose_x(pe, 0, b)

            def group(n, p, i, more):
                g_product(n, p)
                v_product(n, p, 0)
                scores(n, p)
                if more:
                    transpose_x(pe, n + 1, 0)
                    transpose_x(pe, n + 1, 1)
                v_product(n, p, 1)
                if more:
                    transpose_x(pe, n + 1, 2)
                    transpose_x(pe, n + 1, 3)
                v_product(n, p, 2)
                transpose_probs(n)
                v_product(n, p, 3)
                for b in range(GB):
                    output(n, b)

            pairs(pe, s, group, first)

        @block.scalar
        def _(act):
            def sum_squares(n, p, i_load, b):
                if b == 0:
                    act.wait_ge(x_loaded[p], 16 * i_load + 16)
                    wait_used(act, rstd_done, n)
                wait_used(act, summed, GB * n + b)
                nc.scalar.activation(square[:], x_in[p][:, b, :], ACT.Square,
                                     accum_out=sumsq[:, b:b + 1]).then_inc(summed, 1)

            def h_high(n, p, b):
                act.wait_ge(turn_read[b % 2], 2 * n + b // 2 + 1)
                nc.scalar.copy(h_hi[p][:, :, b * P:(b + 1) * P], h[p][:, :, b * P:(b + 1) * P]).then_inc(h_hi_done, 1)

            def v_high(n, b):
                act.wait_ge(ring_full[b], 3 * n + 2)
                nc.scalar.copy(v_hi[:, b, :], ring[b][:]).then_inc(v_hi_done, 1)

            def first():
                for b in range(GB):
                    sum_squares(0, 0, 0, b)
                for b in range(GB):
                    h_high(0, 0, b)

            def group(n, p, i, more):
                for j in range(KD):
                    act.wait_ge(ring_full[j], 3 * n + 1)
                    nc.scalar.activation(g[:, j, :], ring[j][:], ACT.Identity,
                                         bias=keep["wk_bq"][:, j:j + 1]).then_inc(ring_read[j], 1)
                    if more:
                        sum_squares(n + 1, 1 - p, i + p, j)
                v_high(n, 0)
                act.wait_ge(bias_done, n + 1)
                for b in range(GB):
                    nc.scalar.activation(probs[:, b, :], score[:, b, :], ACT.Exp, bias=bias[:, b:b + 1], scale=SCALE,
                                         accum_out=den[:, b:b + 1]).then_inc(exp_done, 1)
                if more:
                    h_high(n + 1, 1 - p, 0)
                    h_high(n + 1, 1 - p, 1)
                v_high(n, 1)
                if more:
                    h_high(n + 1, 1 - p, 2)
                    h_high(n + 1, 1 - p, 3)
                v_high(n, 2)
                act.wait_ge(pT_full, n + 1)
                nc.scalar.copy(pT_hi[:], pT[:]).then_inc(pT_hi_done, 1)
                v_high(n, 3)

            pairs(act, s, group, first)

        @block.vector
        def _(dve):
            def normalize(n, p, b):
                dve.wait_ge(rstd_done, n + 1)
                if b >= 2:
                    wait_used(dve, turn_full[b % 2], 2 * n + b // 2)
                dve.tensor_scalar(x_norm[b % 2][:], x_in[p][:, b, :], rstd[:, b:b + 1], float(D) ** 0.5,
                                  ALU.mult, ALU.mult).then_inc(normed, 1)

            def take_coef(n):
                dve.tensor_copy(coef[:], keep["film"][0][:, :, bass.ds(GB * n, GB)]).then_inc(coef_ready, 1)
                dve.wait_ge(coef_ready, n + 1)

            def modulate(n, p, b):
                dve.wait_ge(turn_full[b % 2], 2 * n + b // 2 + 1)
                for k in range(KD):
                    last = dve.tensor_scalar(h[p][:, k, b * P:(b + 1) * P], turn[b % 2][:, k, :], coef[:, k, b:b + 1],
                                             coef[:, KD + k, b:b + 1], ALU.mult, ALU.add)
                last.then_inc(turn_read[b % 2], 1)

            def h_low(n, p, b):
                dve.wait_ge(h_hi_done, GB * n + b + 1)
                tok = slice(b * P, (b + 1) * P)
                dve.tensor_tensor(h_lo[p][:, :, tok], h[p][:, :, tok], h_hi[p][:, :, tok].bitcast(F32),
                                  ALU.subtract).then_inc(h_lo_done, 1)

            def key_terms(n, p):
                dve.wait_ge(turn_read[1], 2 * n + 2)
                dve.tensor_scalar(key_bias[:], h[p][:, 0, :], keep["wq_bk"][:, 0:1], keep["bq_bk"][:],
                                  ALU.mult, ALU.add).then_inc(key_bias_done, 1)
                for k in range(1, KD):
                    dve.wait_ge(key_bias_done, KD * n + k)
                    dve.scalar_tensor_tensor(key_bias[:], h[p][:, k, :], keep["wq_bk"][:, k:k + 1], key_bias[:],
                                             ALU.mult, ALU.add).then_inc(key_bias_done, 1)

            def v_low(n, b):
                dve.wait_ge(v_hi_done, GB * n + b + 1)
                dve.tensor_tensor(v_lo[:, b, :], ring[b][:], v_hi[:, b, :].bitcast(F32),
                                  ALU.subtract).then_inc(ring_read[b], 1)

            def first():
                normalize(0, 0, 0)
                normalize(0, 0, 1)
                take_coef(0)
                for b in range(GB):
                    modulate(0, 0, b)
                    if b + 2 < GB:
                        normalize(0, 0, b + 2)
                for b in range(GB):
                    h_low(0, 0, b)
                key_terms(0, 0)

            def group(n, p, i, more):
                q = 1 - p
                if more:
                    normalize(n + 1, q, 0)
                    normalize(n + 1, q, 1)
                v_low(n, 0)
                dve.wait_ge(scored, n + 1)
                dve.tensor_reduce(top[:], score[:], AX_X, ALU.max).then_inc(top_done, 1)
                dve.wait_ge(top_done, n + 1)
                dve.tensor_scalar(bias[:], top[:], -SCALE, None, ALU.mult).then_inc(bias_done, 1)
                if more:
                    take_coef(n + 1)
                    modulate(n + 1, q, 0)
                    normalize(n + 1, q, 2)
                    modulate(n + 1, q, 1)
                    normalize(n + 1, q, 3)
                    h_low(n + 1, q, 0)
                    h_low(n + 1, q, 1)
                v_low(n, 1)
                if more:
                    modulate(n + 1, q, 2)
                    modulate(n + 1, q, 3)
                    h_low(n + 1, q, 2)
                    h_low(n + 1, q, 3)
                v_low(n, 2)
                dve.wait_ge(exp_done, GB * n + GB)
                dve.reciprocal(rden[:], den[:]).then_inc(rden_done, 1)
                dve.wait_ge(pT_hi_done, n + 1)
                dve.tensor_tensor(pT_lo[:], pT[:], pT_hi[:].bitcast(F32), ALU.subtract).then_inc(pT_read, 1)
                v_low(n, 3)
                if more:
                    key_terms(n + 1, q)
                dve.wait_ge(rden_done, n + 1)
                dve.wait_ge(biased, n + 1)
                for b in range(GB):
                    dve.wait_ge(ring_full[b], 3 * n + 3)
                    dve.scalar_tensor_tensor(x_in[p][:, b, :], ring[b][:], rden[:, b:b + 1], x_in[p][:, b, :],
                                             ALU.mult, ALU.add).then_inc(ring_read[b], 1)

            pairs(dve, s, group, first)


def mlp_stage(nc, s, w1_dram, w2_dram, x2_dram, out_dram, keep):
    KD, KH, GB, TOK, D, H = s.KD, s.KH, s.GB, s.TOK, s.D, s.H
    with ExitStack() as ctx:
        def sb(name, shape, dt=F32):
            return ctx.enter_context(nc.sbuf_tensor(name, shape, dt))

        def ps(name, shape):
            return ctx.enter_context(nc.psum_tensor(name, shape, F32))

        def sem(name):
            return ctx.enter_context(nc.semaphore("m_" + name))

        def sems(name, n):
            return [sem(f"{name}{i}") for i in range(n)]

        w1_hi, w1_lo = sb("w1_hi", [P, KD, H], F32R), sb("w1_lo", [P, KD, H], F32R)
        w2_hi, w2_lo = sb("w2_hi", [P, KH, D], F32R), sb("w2_lo", [P, KH, D], F32R)
        x_in = [sb(f"mx_in{p}", [P, GB, D]) for p in range(2)]
        x_norm = [sb(f"mx_norm{r}", [P, D]) for r in range(2)]
        square = sb("m_square", [P, D])
        sumsq, rstd = sb("m_sumsq", [P, GB]), sb("m_rstd", [P, GB])
        coef = sb("m_coef", [P, 2 * KD, GB])
        h = [sb(f"mh{r}", [P, KD, P]) for r in range(2)]
        h_hi = [sb(f"mh_hi{p}", [P, KD, TOK], F32R) for p in range(2)]
        h_lo = [sb(f"mh_lo{p}", [P, KD, TOK], F32R) for p in range(2)]
        act_full = [sb(f"m_act{r}", [P, TOK]) for r in range(2)]
        act_hi = [sb(f"m_act_hi{r}", [P, TOK], F32R) for r in range(2)]
        act_lo = [sb(f"m_act_lo{r}", [P, TOK], F32R) for r in range(2)]
        hidden = [ps(f"m_hidden{r}", [P, TOK]) for r in range(2)]
        turn = [ps(f"m_turn{r}", [P, KD, P]) for r in range(2)]
        total = [ps(f"m_total{b}", [P, D]) for b in range(GB)]

        w_loaded, w_hi_done, w_lo_done = sems("w_loaded", 2), sem("w_hi_done"), sems("w_lo_done", 2)
        x_loaded, stored = sems("x_loaded", 2), sems("stored", 2)
        summed, eps_added, rstd_done = sem("summed"), sem("eps_added"), sem("rstd_done")
        normed, biased = sem("normed"), sem("biased")
        turn_full, turn_read = sems("turn_full", 2), sems("turn_read", 2)
        coef_ready, h_hi_done, h_lo_done = sem("coef_ready"), sem("h_hi_done"), sem("h_lo_done")
        hidden_full, hidden_read = sems("hidden_full", 2), sems("hidden_read", 2)
        act_hi_done, act_lo_done, act_used = sems("act_hi_done", 2), sems("act_lo_done", 2), sems("act_used", 2)
        total_full, total_read = sems("total_full", GB), sems("total_read", GB)

        TURN_AT = [5 + 2 * b for b in range(GB)]

        PIECE = GB * D
        pieces = [(w1_hi, w1_lo, w1_dram, k, H) for k in range(KD)]
        per = PIECE // D
        pieces += [(w2_hi, w2_lo, w2_dram, c, None) for c in range(KH // per)]

        def part(w, c, wide):
            if wide:
                return w[:, c, :]
            return w[:, c * per:(c + 1) * per, :].rearrange("p k n -> p (k n)")

        x2_groups = x2_dram.rearrange("(g b) t d -> g t b d", b=GB)
        out_groups = out_dram.rearrange("(g b) t d -> g t b d", b=GB)
        block = ctx.enter_context(nc.Block())

        @block.sync
        def _(sp):
            for t, (_, _, w, c, wide) in enumerate(pieces):
                r = t % 2
                if t >= 2:
                    sp.wait_ge(w_lo_done[r], t // 2)
                src = w[c * P:(c + 1) * P, :] if wide else \
                    w[c * per * P:(c + 1) * per * P, :].rearrange("(k p) n -> p k n", p=P)
                dst = x_in[r][:].rearrange("p b d -> p (b d)") if wide else x_in[r][:]
                sp.dma_start(dst, src).then_inc(w_loaded[r], 16)

            def load(n, p):
                sp.dma_start(x_in[p][:], x2_groups[n]).then_inc(x_loaded[p], 16)

            def group(n, p, i, more):
                for b in range(GB):
                    sp.wait_ge(total_read[b], n + 1)
                sp.dma_start(out_groups[n], x_in[p][:]).then_inc(stored[p], 16)
                sp.wait_ge(stored[p], 16 * i + 16)
                if not isinstance(i, int) or i < s.PAIRS - 1:
                    load(n + 2, p)

            for p in range(2):
                sp.wait_ge(w_lo_done[p], len(pieces) // 2)
                load(p, p)
            pairs(sp, s, group)

        @block.gpsimd
        def _(pool):
            def norm(n, p):
                pool.wait_ge(summed, GB * n + GB)
                nc.gpsimd.tensor_tensor(rstd[:], sumsq[:], keep["eps_sum"][:].broadcast_to([P, GB]),
                                        ALU.add).then_inc(eps_added, 1)
                pool.wait_ge(eps_added, n + 1)
                nc.gpsimd.tensor_tensor(rstd[:], rstd[:], keep["minus_half"][:].broadcast_to([P, GB]),
                                        ALU.pow).then_inc(rstd_done, 1)
                pool.wait_ge(normed, GB * n + GB)
                for b in range(GB):
                    last = nc.gpsimd.tensor_tensor(x_in[p][:, b, :], x_in[p][:, b, :], keep["b2_wide"][:], ALU.add)
                last.then_inc(biased, 1)

            def group(n, p, i, more):
                if more:
                    norm(n + 1, 1 - p)

            pairs(pool, s, group, lambda: norm(0, 0))

        @block.tensor
        def _(pe):
            def transpose_x(n, b):
                r = b % 2
                pe.wait_ge(normed, GB * n + b + 1)
                wait_used(pe, turn_read[r], 2 * n + b // 2)
                for k in range(KD):
                    mm = pe.transpose(turn[r][:, k, :], x_norm[r][:, k * P:(k + 1) * P], keep["ident"][:])
                mm.then_inc(turn_full[r], 1)

            def up(n, p, j):
                if j == 0:
                    pe.wait_ge(h_hi_done, GB * n + GB)
                    pe.wait_ge(h_lo_done, GB * n + GB)
                r = j % 2
                wait_used(pe, hidden_read[r], KH // 2 * n + j // 2)
                steps = [t for k in range(KD) for t in split3(
                    w1_hi[:, k, j * P:(j + 1) * P], w1_lo[:, k, j * P:(j + 1) * P], h_hi[p][:, k, :], h_lo[p][:, k, :])]
                for t, (a, m) in enumerate(steps):
                    mm = pe.matmul(hidden[r][:], a, m, start=t == 0, stop=t == len(steps) - 1)
                mm.then_inc(hidden_full[r], 1)

            def down(n, j):
                r, use = j % 2, KH // 2 * n + j // 2
                pe.wait_ge(act_hi_done[r], use + 1)
                for b in range(GB):
                    tok = slice(b * P, (b + 1) * P)
                    if j == 0:
                        wait_used(pe, total_read[b], n)
                    pe.matmul(total[b][:], act_hi[r][:, tok], w2_hi[:, j, :], start=j == 0, stop=False)
                    pe.matmul(total[b][:], act_hi[r][:, tok], w2_lo[:, j, :], start=False, stop=False)
                pe.wait_ge(act_lo_done[r], use + 1)
                for b in range(GB):
                    mm = pe.matmul(total[b][:], act_lo[r][:, b * P:(b + 1) * P], w2_hi[:, j, :],
                                   start=False, stop=j == KH - 1)
                    if j == KH - 1:
                        mm.then_inc(total_full[b], 1)
                if j < KH - 1:
                    mm.then_inc(act_used[r], 1)

            def first():
                for r in range(2):
                    pe.wait_ge(w_lo_done[r], len(pieces) // 2)
                for b in range(GB):
                    transpose_x(0, b)

            def group(n, p, i, more):
                up(n, p, 0)
                for j in range(KH):
                    if j + 1 < KH:
                        up(n, p, j + 1)
                    down(n, j)
                    if more and j in TURN_AT:
                        transpose_x(n + 1, TURN_AT.index(j))

            pairs(pe, s, group, first)

        @block.scalar
        def _(act):
            for t, (hi, _, _, c, wide) in enumerate(pieces):
                act.wait_ge(w_loaded[t % 2], 16 * (t // 2) + 16)
                nc.scalar.copy(part(hi, c, wide), x_in[t % 2][:].rearrange("p b d -> p (b d)")).then_inc(w_hi_done, 1)

            def sum_squares(n, p, i_load):
                act.wait_ge(x_loaded[p], 16 * i_load + 16)
                wait_used(act, rstd_done, n)
                for b in range(GB):
                    wait_used(act, summed, GB * n + b)
                    nc.scalar.activation(square[:], x_in[p][:, b, :], ACT.Square,
                                         accum_out=sumsq[:, b:b + 1]).then_inc(summed, 1)

            def h_high(n, p, b):
                act.wait_ge(turn_read[b % 2], 2 * n + b // 2 + 1)
                nc.scalar.copy(h_hi[p][:, :, b * P:(b + 1) * P], h[b % 2][:]).then_inc(h_hi_done, 1)

            def gelu(n, j):
                r, use = j % 2, KH // 2 * n + j // 2
                act.wait_ge(hidden_full[r], use + 1)
                if r == 0:
                    wait_used(act, act_used[0], use)
                elif j == 1:
                    wait_used(act, total_full[GB - 1], n)
                else:
                    act.wait_ge(act_used[1], (KH // 2 - 1) * n + j // 2)
                b1 = keep["cols"][:, keep["b1_at"] + j:keep["b1_at"] + j + 1]
                nc.scalar.activation(act_hi[r][:], hidden[r][:], ACT.Gelu, bias=b1).then_inc(act_hi_done[r], 1)
                nc.scalar.activation(act_full[r][:], hidden[r][:], ACT.Gelu, bias=b1).then_inc(hidden_read[r], 1)

            def first():
                sum_squares(0, 0, 0)
                for b in range(GB):
                    h_high(0, 0, b)

            def group(n, p, i, more):
                for j in range(KH):
                    gelu(n, j)
                    if more and j == 3:
                        sum_squares(n + 1, 1 - p, i + p)
                    if more and j - 2 in TURN_AT:
                        h_high(n + 1, 1 - p, TURN_AT.index(j - 2))

            pairs(act, s, group, first)

        @block.vector
        def _(dve):
            for t, (hi, lo, _, c, wide) in enumerate(pieces):
                dve.wait_ge(w_hi_done, t + 1)
                dve.tensor_tensor(part(lo, c, wide), x_in[t % 2][:].rearrange("p b d -> p (b d)"),
                                  part(hi, c, wide).bitcast(F32), ALU.subtract).then_inc(w_lo_done[t % 2], 1)

            def normalize(n, p, b):
                dve.wait_ge(rstd_done, n + 1)
                if b >= 2:
                    wait_used(dve, turn_full[b % 2], 2 * n + b // 2)
                dve.tensor_scalar(x_norm[b % 2][:], x_in[p][:, b, :], rstd[:, b:b + 1], float(D) ** 0.5,
                                  ALU.mult, ALU.mult).then_inc(normed, 1)

            def take_coef(n):
                dve.tensor_copy(coef[:], keep["film"][1][:, :, bass.ds(GB * n, GB)]).then_inc(coef_ready, 1)
                dve.wait_ge(coef_ready, n + 1)

            def modulate(n, b):
                dve.wait_ge(turn_full[b % 2], 2 * n + b // 2 + 1)
                for k in range(KD):
                    last = dve.tensor_scalar(h[b % 2][:, k, :], turn[b % 2][:, k, :], coef[:, k, b:b + 1],
                                             coef[:, KD + k, b:b + 1], ALU.mult, ALU.add)
                last.then_inc(turn_read[b % 2], 1)

            def h_low(n, p, b):
                dve.wait_ge(h_hi_done, GB * n + b + 1)
                tok = slice(b * P, (b + 1) * P)
                dve.tensor_tensor(h_lo[p][:, :, tok], h[b % 2][:], h_hi[p][:, :, tok].bitcast(F32),
                                  ALU.subtract).then_inc(h_lo_done, 1)

            def first():
                normalize(0, 0, 0)
                normalize(0, 0, 1)
                take_coef(0)
                for b in range(GB):
                    modulate(0, b)
                    if b + 2 < GB:
                        normalize(0, 0, b + 2)
                    h_low(0, 0, b)

            def group(n, p, i, more):
                for j in range(KH):
                    r, use = j % 2, KH // 2 * n + j // 2
                    dve.wait_ge(hidden_read[r], use + 1)
                    dve.tensor_tensor(act_lo[r][:], act_full[r][:], act_hi[r][:].bitcast(F32),
                                      ALU.subtract).then_inc(act_lo_done[r], 1)
                    if more and j == TURN_AT[0] - 1:
                        normalize(n + 1, 1 - p, 0)
                        normalize(n + 1, 1 - p, 1)
                        take_coef(n + 1)
                    if more and j - 1 in TURN_AT:
                        b = TURN_AT.index(j - 1)
                        modulate(n + 1, b)
                        if b + 2 < GB:
                            normalize(n + 1, 1 - p, b + 2)
                    if more and j - 2 in TURN_AT:
                        h_low(n + 1, 1 - p, TURN_AT.index(j - 2))
                dve.wait_ge(biased, n + 1)
                for b in range(GB):
                    dve.wait_ge(total_full[b], n + 1)
                    dve.tensor_tensor(x_in[p][:, b, :], total[b][:], x_in[p][:, b, :],
                                      ALU.add).then_inc(total_read[b], 1)

            pairs(dve, s, group, first)


def cond_block_kernel(nc, x, cols, rows, condT, wqT, wkT, wvT, wp, f1w, f2w, w1, w2, out, x2):
    s = Shapes(x, w1)
    cmap, _ = column_map(s)
    with ExitStack() as ctx:
        def sb(name, shape, dt=F32):
            return ctx.enter_context(nc.sbuf_tensor(name, shape, dt))

        keep = {
            "cols": sb("cols", [P, cols.shape[1]]),
            "ident": sb("ident", [P, P]),
            "minus_half": sb("minus_half", [P, 1]),
            "eps_sum": sb("eps_sum", [P, 1]),
            "b2_wide": sb("b2_wide", [P, s.D]),
            "film": [sb(f"film_coef{f}", [P, 2 * s.KD, s.B]) for f in range(2)],
            "b1_at": cmap["b1"][0],
        }
        with ExitStack() as attn:
            def asb(name, shape, dt=F32):
                return attn.enter_context(nc.sbuf_tensor(name, shape, dt))

            keep |= {
                "ones": asb("ones", [P, P]),
                "attn_bias": asb("attn_bias", [P, s.D]),
                "wk_bq": asb("wk_bq", [P, s.KD]),
                "wq_bk": asb("wq_bk", [P, s.KD]),
                "bq_bk": asb("bq_bk", [P, 1]),
                "bq_bk_terms": asb("bq_bk_terms", [P, s.KD]),
            }
            keep |= {n: asb(n, [P, s.KD, s.D], F32R) for n in ("qk_hi", "qk_lo", "vp_hi", "vp_lo")}
            dram = {"cols": cols, "rows": rows, "condT": condT, "wqT": wqT, "wkT": wkT, "wvT": wvT, "wp": wp,
                    "f1w": f1w, "f2w": f2w}
            setup_stage(nc, s, dram, keep, cmap)
            attention_stage(nc, s, x, x2, keep)
        mlp_stage(nc, s, w1, w2, x2, out, keep)


def kernel(**inputs):
    import numpy as np
    import concourse.bacc as bacc
    from concourse.bass_utils import run_bass_kernel_spmd

    def get(name):
        return np.asarray(inputs["L0_cond_" + name])

    def columns(v):
        return v.reshape(-1, P).T

    packed = np.concatenate([columns(get(n)) for n in (
        "norm1_w", "film1_b", "q_b", "k_b", "v_b", "norm2_w", "film2_b", "mlp_b1")], axis=1)
    arrays = {
        "x": np.asarray(inputs["x"]),
        "cols": packed,
        "rows": np.stack([get("proj_b"), get("mlp_b2")]),
        "condT": np.asarray(inputs["cond_1024"]).T,
        "wqT": get("q_w").T, "wkT": get("k_w").T, "wvT": get("v_w").T, "wp": get("proj_w"),
        "f1w": get("film1_w"), "f2w": get("film2_w"), "w1": get("mlp_w1"), "w2": get("mlp_w2"),
    }
    arrays = {f"{k}_dram": np.ascontiguousarray(v) for k, v in arrays.items()}
    nc = bacc.Bacc("TRN2", target_bir_lowering=False, num_devices=1)
    args = [nc.dram_tensor(k, v.shape, mybir.dt.from_np(v.dtype), kind="ExternalInput").ap()
            for k, v in arrays.items()]
    shape = arrays["x_dram"].shape
    out = nc.dram_tensor("out_dram", shape, F32, kind="ExternalOutput").ap()
    x2 = nc.dram_tensor("x2_scratch", shape, F32, kind="Internal").ap()
    cond_block_kernel(nc, *args, out, x2)
    result = run_bass_kernel_spmd(nc, [arrays], core_ids=[0])
    return result.results[0]["out_dram"]
```

```python
from contextlib import ExitStack

import concourse.bass as bass
from concourse import mybir

F32 = mybir.dt.float32
F32R = mybir.dt.float32r
BF16 = mybir.dt.bfloat16
ACT = mybir.ActivationFunctionType
ALU = mybir.AluOpType
AX_X = mybir.AxisListType.X

P = 128
EPS = 1e-6
GB = 4
TOK = GB * P
STAGE = 2


def column_map(KD, KH):
    at, out = 0, {}
    for name, n in (("n1", KD), ("f1b", 2 * KD), ("bq", KD), ("bk", KD), ("bv", KD),
                    ("n2", KD), ("f2b", 2 * KD), ("b1", KH)):
        out[name] = (at, at + n)
        at += n
    return out


def split3(hi_a, lo_a, hi_b, lo_b):
    return ((hi_a, hi_b), (hi_a, lo_b), (lo_a, hi_b))


def wait_used(engine, sem, uses):
    if not isinstance(uses, int) or uses > 0:
        engine.wait_ge(sem, uses)


def group_pairs(engine, pairs, body):
    for p in range(2):
        body(p, p, 0)
    with engine.Fori(1, pairs - 1) as i:
        for p in range(2):
            body(2 * i + p, p, i)
    for p in range(2):
        body(2 * (pairs - 1) + p, p, pairs - 1)


def cond_block_kernel(nc, x, cols, rows, condT, wqT, wkT, wvT, wp, f1w, f2w, w1, w2, out, x2):
    B, N, D = x.shape
    H = w1.shape[1]
    KD, KH = D // P, H // P
    GROUPS = B // GB
    PAIRS = GROUPS // 2
    SCALE = float(D) ** -0.5
    assert N == P and KD == GB and D == TOK and KH % 4 == 0
    cmap = column_map(KD, KH)

    with ExitStack() as ctx:
        def tensor(stack, name, shape, dt=F32):
            return stack.enter_context(nc.sbuf_tensor(name, shape, dt))

        def sem(name):
            return ctx.enter_context(nc.semaphore(name))

        def sems(name, n):
            return [sem(f"{name}{i}") for i in range(n)]

        def keep(name, shape, dt=F32):
            return tensor(ctx, name, shape, dt)

        vecs = keep("vecs", [P, cols.shape[1]])
        ident = keep("ident", [P, P])
        minus_half, eps_sum = keep("minus_half", [P, 1]), keep("eps_sum", [P, 1])
        b2_wide = keep("b2_wide", [P, D])
        film2 = keep("film2", [P, 2 * KD, B])
        x_in = [keep(f"x_in{p}", [P, GB, D]) for p in range(2)]
        x_norm = [keep(f"x_norm{r}", [P, D]) for r in range(2)]
        square = keep("square", [P, D], BF16)
        sumsq, rstd = keep("sumsq", [P, GB]), keep("rstd", [P, GB])
        coef = keep("coef", [P, 2 * KD, GB])
        h_hi = [keep(f"h_hi{p}", [P, KD, TOK], F32R) for p in range(2)]
        h_lo = [keep(f"h_lo{p}", [P, KD, TOK], F32R) for p in range(2)]
        h_mlp = [keep(f"h_mlp{r}", [P, KD, P]) for r in range(2)]
        stage = [keep(f"stage{r}", [P, D]) for r in range(STAGE)]

        with ExitStack() as early:
            wqT_sb, wkT_sb, wvT_sb, wp_sb = (tensor(early, n, [P, KD, D]) for n in ("wqT", "wkT", "wvT", "wp"))
            f1w_sb, f2w_sb = (tensor(early, n, [P, KD, 2 * D]) for n in ("f1w", "f2w"))
        w1_hi, w1_lo = keep("w1_hi", [P, KD, H], F32R), keep("w1_lo", [P, KD, H], F32R)

        with ExitStack() as attn:
            def own(name, shape, dt=F32):
                return tensor(attn, name, shape, dt)

            qk_hi, qk_lo, vp_hi, vp_lo = (own(n, [P, KD, D], F32R) for n in ("qk_hi", "qk_lo", "vp_hi", "vp_lo"))
            film1 = own("film1", [P, 2 * KD, B])
            ones = own("ones", [P, P])
            attn_bias = own("attn_bias", [P, D])
            wk_bq, wq_bk, bq_bk_terms = (own(n, [P, KD]) for n in ("wk_bq", "wq_bk", "bq_bk_terms"))
            bq_bk = own("bq_bk", [P, 1])
            h = own("h", [P, KD, TOK])
            key_bias = own("key_bias", [P, TOK])
            v_hi, v_lo = own("v_hi", [P, GB, D], F32R), own("v_lo", [P, GB, D], F32R)
            probs = own("probs", [P, GB, P])
            top, exp_bias, den, rden = (own(n, [P, GB]) for n in ("top", "exp_bias", "den", "rden"))
            pT_hi, pT_lo = own("pT_hi", [P, TOK], F32R), own("pT_lo", [P, TOK], F32R)
            with ExitStack() as early:
                condT_sb = tensor(early, "condT", [P, KD, B])
                bv_wide = tensor(early, "bv_wide", [P, KD, P])
                bp_wide = tensor(early, "bp_wide", [P, D])
                one_plus = tensor(early, "one_plus", [P, 2, KD])
            g = own("g", [P, KD, TOK])
        w2_hi, w2_lo = keep("w2_hi", [P, KH, D], F32R), keep("w2_lo", [P, KH, D], F32R)
        act_full = [keep(f"act_full{r}", [P, TOK]) for r in range(2)]
        act_hi = [keep(f"act_hi{r}", [P, TOK], F32R) for r in range(2)]
        act_lo = [keep(f"act_lo{r}", [P, TOK], F32R) for r in range(2)]

        def bank(name, shape):
            return ctx.enter_context(nc.psum_tensor(name, shape, F32))

        ring = [bank(f"ring{r}", [P, D]) for r in range(4)]
        turn = [bank(f"turn{r}", [P, KD, P]) for r in range(2)]
        score = bank("score", [P, GB, P])
        pT = bank("pT", [P, TOK])
        vec = score[:].rearrange("p b t -> p (b t)")
        film_ps = pT[:].rearrange("p (j b) -> p j b", j=2 * KD)
        hidden = [vec, pT[:]]

        loads = ("vecs", "condT", "wqT", "wkT", "wvT", "wp", "f1w", "f2w", "bp", "b2")
        loaded = {n: sem("loaded_" + n) for n in loads}
        ident_zero, ident_done, const_done, bv_wide_done = (
            sem(n) for n in ("ident_zero", "ident_done", "const_done", "bv_wide_done"))
        prod_full, prod_hi, prod_lo = (sems(n, KD) for n in ("prod_full", "prod_hi", "prod_lo"))
        vec_full, vec_read, row_full, row_read = (sem(n) for n in ("vec_full", "vec_read", "row_full", "row_read"))
        film_full, film_read, one_plus_done, bq_bk_done = (
            sem(n) for n in ("film_full", "film_read", "one_plus_done", "bq_bk_done"))
        x_loaded, stored = sems("x_loaded", 2), sems("stored", 2)
        summed, eps_added, rstd_done, normed, biased = (
            sem(n) for n in ("summed", "eps_added", "rstd_done", "normed", "biased"))
        turn_full, turn_read = sems("turn_full", 2), sems("turn_read", 2)
        coef_ready, h_hi_done, h_lo_done = sem("coef_ready"), sem("h_hi_done"), sem("h_lo_done")
        ring_full, ring_read = sems("ring_full", 4), sems("ring_read", 4)
        key_bias_done, v_hi_done, scored, top_done, bias_done, exp_done = (
            sem(n) for n in ("key_bias_done", "v_hi_done", "scored", "top_done", "bias_done", "exp_done"))
        pT_full, pT_hi_done, pT_read, rden_done = (sem(n) for n in ("pT_full", "pT_hi_done", "pT_read", "rden_done"))
        piece_loaded, piece_hi, pieces_split = sems("piece_loaded", STAGE), sem("piece_hi"), sem("pieces_split")
        hidden_full, hidden_read = sems("hidden_full", 2), sems("hidden_read", 2)
        act_hi_done, act_lo_done, act_used = sems("act_hi_done", 2), sems("act_lo_done", 2), sems("act_used", 2)
        total_full, total_read = sems("total_full", GB), sems("total_read", GB)

        x_groups, x2_groups, out_groups = (a.rearrange("(g b) t d -> g t b d", b=GB) for a in (x, x2, out))

        def col(name):
            a, b = cmap[name]
            return vecs[:, a:b]

        def tokens(b):
            return slice(b * P, (b + 1) * P)

        def piece(w_1, w_2, t):
            if t < KH:
                return w_1[:, :, t * P:(t + 1) * P]
            return w_2[:, t - KH, :].rearrange("p (a n) -> p a n", a=KD)

        def stage_of(t):
            return stage[t % STAGE][:].rearrange("p (a n) -> p a n", a=KD)

        TURN_AT = [5 + 2 * b for b in range(GB)]
        SUM_AT = 3
        block = ctx.enter_context(nc.Block())

        @block.sync
        def _(sp):
            def chunked(a):
                return a.rearrange("(k p) n -> p k n", p=P)

            def load(m, use_source, p):
                sp.dma_start(x_in[p][:], use_source[m]).then_inc(x_loaded[p], 16)

            def load_piece(t):
                if t >= STAGE:
                    sp.wait_ge(pieces_split, t - STAGE + 1)
                if t < KH:
                    src = w1[:, t * P:(t + 1) * P].rearrange("(k p) n -> p k n", p=P)
                else:
                    src = w2[(t - KH) * P:(t - KH + 1) * P, :].rearrange("p (a n) -> p a n", a=KD)
                sp.dma_start(stage_of(t), src).then_inc(piece_loaded[t % STAGE], 16)

            sp.dma_start(wqT_sb[:], chunked(wqT)).then_inc(loaded["wqT"], 16)
            sp.dma_start(wkT_sb[:], chunked(wkT)).then_inc(loaded["wkT"], 16)
            sp.dma_start(vecs[:], cols).then_inc(loaded["vecs"], 16)
            sp.dma_start(condT_sb[:], chunked(condT)).then_inc(loaded["condT"], 16)
            sp.dma_start(f1w_sb[:], chunked(f1w)).then_inc(loaded["f1w"], 16)
            load(0, x_groups, 0)
            sp.dma_start(wvT_sb[:], chunked(wvT)).then_inc(loaded["wvT"], 16)
            sp.dma_start(wp_sb[:], chunked(wp)).then_inc(loaded["wp"], 16)
            sp.dma_start(bp_wide[:], rows[0:1, :].broadcast_to([P, D])).then_inc(loaded["bp"], 16)
            sp.dma_start(b2_wide[:], rows[1:2, :].broadcast_to([P, D])).then_inc(loaded["b2"], 16)
            sp.dma_start(f2w_sb[:], chunked(f2w)).then_inc(loaded["f2w"], 16)
            load(1, x_groups, 1)

            def attention(n, p, i):
                if isinstance(i, int) and i == 0:
                    for t in range(n * KH // 2, (n + 1) * KH // 2):
                        load_piece(t)
                if isinstance(i, int) and n == GROUPS - 1:
                    for t in range(KH, KH + STAGE):
                        load_piece(t)
                for b in range(GB):
                    sp.wait_ge(ring_read[b], 3 * n + 3)
                sp.dma_start(x2_groups[n], x_in[p][:]).then_inc(stored[p], 16)
                if isinstance(i, int) and n == GROUPS - 1:
                    for t in range(KH + STAGE, KH + 2 * STAGE):
                        load_piece(t)
                sp.wait_ge(stored[p], 16 * i + 16)
                if isinstance(i, int) and i == PAIRS - 1:
                    load(p, x2_groups, p)
                else:
                    load(n + 2, x_groups, p)

            def mlp(n, p, i):
                if isinstance(n, int) and n == 0:
                    for t in range(KH + 2 * STAGE, 2 * KH):
                        load_piece(t)
                for b in range(GB):
                    sp.wait_ge(total_read[b], n + 1)
                sp.dma_start(out_groups[n], x_in[p][:]).then_inc(stored[p], 16)
                sp.wait_ge(stored[p], 16 * (PAIRS + i) + 16)
                if not (isinstance(i, int) and i == PAIRS - 1):
                    load(n + 2, x2_groups, p)

            group_pairs(sp, PAIRS, attention)
            group_pairs(sp, PAIRS, mlp)

        @block.gpsimd
        def _(pool):
            nc.gpsimd.memset(ident[:], 0.0).then_inc(ident_zero, 1)
            pool.wait_ge(ident_zero, 1)
            nc.gpsimd.affine_select(out=ident[:], in_=ident[:], compare_op=ALU.not_equal, fill=1.0,
                                    base=0, pattern=[[-1, P]], channel_multiplier=1).then_inc(ident_done, 1)
            nc.gpsimd.memset(ones[:], 1.0).then_inc(const_done, 1)
            nc.gpsimd.memset(minus_half[:], -0.5).then_inc(const_done, 1)
            nc.gpsimd.memset(eps_sum[:], EPS * D).then_inc(const_done, 1)
            pool.wait_ge(const_done, 3)

            def norm(m):
                pool.wait_ge(summed, GB * m + GB)
                nc.gpsimd.tensor_tensor(rstd[:], sumsq[:], eps_sum[:].broadcast_to([P, GB]),
                                        ALU.add).then_inc(eps_added, 1)
                pool.wait_ge(eps_added, m + 1)
                nc.gpsimd.tensor_tensor(rstd[:], rstd[:], minus_half[:].broadcast_to([P, GB]),
                                        ALU.pow).then_inc(rstd_done, 1)

            def add_bias(m, p, row):
                pool.wait_ge(normed, GB * m + GB)
                for b in range(GB):
                    last = nc.gpsimd.tensor_tensor(x_in[p][:, b, :], x_in[p][:, b, :], row[:], ALU.add)
                last.then_inc(biased, 1)

            def split_piece(t):
                pool.wait_ge(piece_loaded[t % STAGE], 16 * (t // STAGE) + 16)
                nc.gpsimd.tensor_copy(piece(w1_hi, w2_hi, t), stage_of(t)).then_inc(piece_hi, 1)
                pool.wait_ge(piece_hi, t + 1)
                nc.gpsimd.tensor_tensor(piece(w1_lo, w2_lo, t), stage_of(t), piece(w1_hi, w2_hi, t).bitcast(F32),
                                        ALU.subtract).then_inc(pieces_split, 1)

            def attention(n, p, i):
                mine = []
                if isinstance(i, int) and i == 0:
                    mine = list(range(n * KH // 2, (n + 1) * KH // 2))
                for t in mine[:KH // 4]:
                    split_piece(t)
                norm(n + 1)
                add_bias(n + 1, 1 - p, b2_wide if isinstance(n, int) and n == GROUPS - 1 else attn_bias)
                for t in mine[KH // 4:]:
                    split_piece(t)

            def mlp(n, p, i):
                late = []
                if isinstance(n, int) and n == 0:
                    for b in range(GB):
                        pool.wait_ge(ring_read[b], 3 * GROUPS)
                    for t in range(KH, KH + KH // 2):
                        split_piece(t)
                    late = range(KH + KH // 2, 2 * KH)
                if not (isinstance(n, int) and n == GROUPS - 1):
                    norm(GROUPS + n + 1)
                    for t in late:
                        split_piece(t)
                    add_bias(GROUPS + n + 1, 1 - p, b2_wide)

            norm(0)
            pool.wait_ge(row_read, 1)
            pool.wait_ge(loaded["b2"], 16)
            add_bias(0, 0, attn_bias)
            pool.wait_ge(film_full, 2)
            group_pairs(pool, PAIRS, attention)
            group_pairs(pool, PAIRS, mlp)

        @block.tensor
        def _(pe):
            def product(bank_ap, steps, full):
                for t, (a, b) in enumerate(steps):
                    mm = pe.matmul(bank_ap, a, b, start=t == 0, stop=t == len(steps) - 1)
                if full is not None:
                    mm.then_inc(full, 1)

            def transpose_x(m, b):
                r = b % 2
                pe.wait_ge(normed, GB * m + b + 1)
                wait_used(pe, turn_read[r], 2 * m + b // 2)
                for k in range(KD):
                    mm = pe.transpose(turn[r][:, k, :], x_norm[r][:, k * P:(k + 1) * P], ident[:])
                mm.then_inc(turn_full[r], 1)

            def film_product(w, name):
                pe.wait_ge(loaded[name], 16)
                for j in range(2 * KD):
                    product(film_ps[:, j, :], [(w[:, k, tokens(j)], condT_sb[:, k, :]) for k in range(KD)],
                            film_full if j == 2 * KD - 1 else None)

            def setup():
                pe.wait_ge(loaded["wqT"], 16)
                pe.wait_ge(loaded["wkT"], 16)
                for c in range(KD):
                    product(ring[c][:], [(wqT_sb[:, k, tokens(c)], wkT_sb[:, k, :]) for k in range(KD)], prod_full[c])
                pe.wait_ge(loaded["condT"], 16)
                film_product(f1w_sb, "f1w")
                pe.wait_ge(loaded["vecs"], 16)
                for v, (w, b) in enumerate(((wkT_sb, "bq"), (wqT_sb, "bk"))):
                    for c in range(KD):
                        product(vec[:, v * KD + c:v * KD + c + 1],
                                [(w[:, k, tokens(c)], col(b)[:, k:k + 1]) for k in range(KD)],
                                vec_full if (v, c) == (1, KD - 1) else None)
                pe.wait_ge(ident_done, 1)
                transpose_x(0, 0)
                transpose_x(0, 1)
                pe.wait_ge(loaded["wvT"], 16)
                pe.wait_ge(loaded["wp"], 16)
                for c in range(KD):
                    if c == 2:
                        transpose_x(0, 2)
                        transpose_x(0, 3)
                    pe.wait_ge(prod_lo[c], 1)
                    product(ring[c][:], [(wvT_sb[:, k, tokens(c)], wp_sb[:, k, :]) for k in range(KD)], prod_full[c])
                pe.wait_ge(bv_wide_done, 1)
                pe.wait_ge(vec_read, 2)
                product(vec, [(bv_wide[:, k, :], wp_sb[:, k, :]) for k in range(KD)], row_full)
                pe.wait_ge(film_read, 2 * KD)
                film_product(f2w_sb, "f2w")
                for c in range(KD):
                    pe.wait_ge(prod_lo[c], 2)

            def g_product(n, p):
                pe.wait_ge(h_hi_done, GB * n + GB)
                pe.wait_ge(h_lo_done, GB * n + GB)
                for j in range(KD):
                    wait_used(pe, ring_read[j], 3 * n)
                    product(ring[j][:], [t for k in range(KD) for t in split3(
                        qk_hi[:, k, tokens(j)], qk_lo[:, k, tokens(j)], h_hi[p][:, k, :], h_lo[p][:, k, :])],
                        ring_full[j])

            def v_product(n, p, b):
                pe.wait_ge(ring_read[b], 3 * n + 1)
                product(ring[b][:], [t for k in range(KD) for t in split3(
                    h_hi[p][:, k, tokens(b)], h_lo[p][:, k, tokens(b)], vp_hi[:, k, :], vp_lo[:, k, :])], ring_full[b])

            def scores(n):
                for j in range(KD):
                    pe.wait_ge(ring_read[j], 3 * n + 1)
                pe.wait_ge(key_bias_done, KD * n + KD)
                if isinstance(n, int) and n == 0:
                    pe.wait_ge(row_read, 1)
                    pe.wait_ge(const_done, 3)
                wait_used(pe, exp_done, GB * n)
                for b in range(GB):
                    product(score[:, b, :],
                            [(g[:, k, tokens(b)], h[:, k, tokens(b)]) for k in range(KD)]
                            + [(key_bias[:, tokens(b)], ones[:])], scored if b == GB - 1 else None)

            def transpose_probs(n):
                pe.wait_ge(exp_done, GB * n + GB)
                if isinstance(n, int) and n == 0:
                    pe.wait_ge(film_read, 4 * KD)
                wait_used(pe, pT_read, n)
                for b in range(GB):
                    mm = pe.transpose(pT[:, tokens(b)], probs[:, b, :], ident[:])
                mm.then_inc(pT_full, 1)

            def output(n, b):
                pe.wait_ge(pT_read, n + 1)
                pe.wait_ge(ring_read[b], 3 * n + 2)
                product(ring[b][:], split3(pT_hi[:, tokens(b)], pT_lo[:, tokens(b)], v_hi[:, b, :], v_lo[:, b, :]),
                        ring_full[b])

            def attention(n, p, i):
                g_product(n, p)
                v_product(n, p, 0)
                scores(n)
                v_product(n, p, 1)
                transpose_x(n + 1, 0)
                transpose_x(n + 1, 1)
                v_product(n, p, 2)
                transpose_x(n + 1, 2)
                transpose_x(n + 1, 3)
                transpose_probs(n)
                v_product(n, p, 3)
                for b in range(GB):
                    output(n, b)

            def up(n, p, j):
                if j == 0:
                    pe.wait_ge(h_hi_done, GB * (GROUPS + n) + GB)
                    pe.wait_ge(h_lo_done, GB * (GROUPS + n) + GB)
                    if isinstance(n, int) and n == 0:
                        pe.wait_ge(exp_done, GB * GROUPS)
                        pe.wait_ge(pT_read, GROUPS)
                        pe.wait_ge(pieces_split, KH)
                wait_used(pe, hidden_read[j % 2], KH // 2 * n + j // 2)
                product(hidden[j % 2], [t for k in range(KD) for t in split3(
                    w1_hi[:, k, tokens(j)], w1_lo[:, k, tokens(j)], h_hi[p][:, k, :], h_lo[p][:, k, :])],
                    hidden_full[j % 2])

            def down(n, j):
                r, use = j % 2, KH // 2 * n + j // 2
                pe.wait_ge(act_hi_done[r], use + 1)
                if isinstance(n, int) and n == 0:
                    pe.wait_ge(pieces_split, KH + j + 1)
                for b in range(GB):
                    if j == 0:
                        wait_used(pe, total_read[b], n)
                    pe.matmul(ring[b][:], act_hi[r][:, tokens(b)], w2_hi[:, j, :], start=j == 0, stop=False)
                    pe.matmul(ring[b][:], act_hi[r][:, tokens(b)], w2_lo[:, j, :], start=False, stop=False)
                pe.wait_ge(act_lo_done[r], use + 1)
                for b in range(GB):
                    mm = pe.matmul(ring[b][:], act_lo[r][:, tokens(b)], w2_hi[:, j, :],
                                   start=False, stop=j == KH - 1)
                    if j == KH - 1:
                        mm.then_inc(total_full[b], 1)
                if j < KH - 1:
                    mm.then_inc(act_used[r], 1)

            def mlp(n, p, i):
                last = isinstance(n, int) and n == GROUPS - 1
                up(n, p, 0)
                for j in range(KH):
                    if j + 1 < KH:
                        up(n, p, j + 1)
                    down(n, j)
                    if not last and j in TURN_AT:
                        transpose_x(GROUPS + n + 1, TURN_AT.index(j))

            setup()
            group_pairs(pe, PAIRS, attention)
            group_pairs(pe, PAIRS, mlp)

        @block.scalar
        def _(act):
            def sum_squares(m, p, use):
                act.wait_ge(x_loaded[p], 16 * use + 16)
                wait_used(act, rstd_done, m)
                for b in range(GB):
                    wait_used(act, summed, GB * m + b)
                    nc.scalar.activation(square[:], x_in[p][:, b, :], ACT.Square,
                                         accum_out=sumsq[:, b:b + 1]).then_inc(summed, 1)

            def h_high(m, p, b, source):
                act.wait_ge(turn_read[b % 2], 2 * m + b // 2 + 1)
                nc.scalar.copy(h_hi[p][:, :, tokens(b)], source).then_inc(h_hi_done, 1)

            def h_attn(b):
                return h[:, :, tokens(b)]

            def h_of_next(n, b):
                return h_mlp[b % 2][:] if isinstance(n, int) and n == GROUPS - 1 else h_attn(b)

            def high_part(w, hi, c):
                act.wait_ge(prod_full[c], w + 1)
                nc.scalar.copy(hi[:, c, :], ring[c][:]).then_inc(prod_hi[c], 1)

            def v_high(n, b):
                act.wait_ge(ring_full[b], 3 * n + 2)
                nc.scalar.copy(v_hi[:, b, :], ring[b][:]).then_inc(v_hi_done, 1)

            def attention(n, p, i):
                for j in range(KD):
                    act.wait_ge(ring_full[j], 3 * n + 1)
                    nc.scalar.activation(g[:, j, :], ring[j][:], ACT.Identity,
                                         bias=wk_bq[:, j:j + 1]).then_inc(ring_read[j], 1)
                sum_squares(n + 1, 1 - p, i + p)
                v_high(n, 0)
                act.wait_ge(bias_done, n + 1)
                for b in range(GB):
                    nc.scalar.activation(probs[:, b, :], score[:, b, :], ACT.Exp, bias=exp_bias[:, b:b + 1],
                                         scale=SCALE, accum_out=den[:, b:b + 1]).then_inc(exp_done, 1)
                v_high(n, 1)
                h_high(n + 1, 1 - p, 0, h_of_next(n, 0))
                h_high(n + 1, 1 - p, 1, h_of_next(n, 1))
                v_high(n, 2)
                act.wait_ge(pT_full, n + 1)
                nc.scalar.copy(pT_hi[:], pT[:]).then_inc(pT_hi_done, 1)
                h_high(n + 1, 1 - p, 2, h_of_next(n, 2))
                h_high(n + 1, 1 - p, 3, h_of_next(n, 3))
                v_high(n, 3)

            def gelu(n, j):
                r, use = j % 2, KH // 2 * n + j // 2
                act.wait_ge(hidden_full[r], use + 1)
                if r == 0:
                    wait_used(act, act_used[0], use)
                elif j == 1:
                    wait_used(act, total_full[GB - 1], n)
                else:
                    act.wait_ge(act_used[1], (KH // 2 - 1) * n + j // 2)
                b1 = col("b1")[:, j:j + 1]
                nc.scalar.activation(act_hi[r][:], hidden[r], ACT.Gelu, bias=b1).then_inc(act_hi_done[r], 1)
                nc.scalar.activation(act_full[r][:], hidden[r], ACT.Gelu, bias=b1).then_inc(hidden_read[r], 1)

            def mlp(n, p, i):
                last = isinstance(n, int) and n == GROUPS - 1
                if isinstance(n, int) and n == 0:
                    for b in range(GB):
                        act.wait_ge(ring_read[b], 3 * GROUPS)
                for j in range(KH):
                    gelu(n, j)
                    if not last and j == SUM_AT:
                        sum_squares(GROUPS + n + 1, 1 - p, PAIRS + i + p)
                    if not last and j - 2 in TURN_AT:
                        b = TURN_AT.index(j - 2)
                        h_high(GROUPS + n + 1, 1 - p, b, h_mlp[b % 2][:])

            for c in range(KD):
                high_part(0, qk_hi, c)
            sum_squares(0, 0, 0)
            h_high(0, 0, 0, h_attn(0))
            h_high(0, 0, 1, h_attn(1))
            high_part(1, vp_hi, 0)
            high_part(1, vp_hi, 1)
            h_high(0, 0, 2, h_attn(2))
            h_high(0, 0, 3, h_attn(3))
            high_part(1, vp_hi, 2)
            high_part(1, vp_hi, 3)
            act.wait_ge(vec_read, 2)
            act.wait_ge(row_read, 1)
            act.wait_ge(film_read, 4 * KD)
            group_pairs(act, PAIRS, attention)
            group_pairs(act, PAIRS, mlp)

        @block.vector
        def _(dve):
            def normalize(m, p, b):
                dve.wait_ge(rstd_done, m + 1)
                wait_used(dve, turn_full[b % 2], 2 * m + b // 2)
                dve.tensor_scalar(x_norm[b % 2][:], x_in[p][:, b, :], rstd[:, b:b + 1], float(D) ** 0.5,
                                  ALU.mult, ALU.mult).then_inc(normed, 1)

            def take_coef(m, film, group):
                dve.tensor_copy(coef[:], film[:, :, bass.ds(GB * group, GB)]).then_inc(coef_ready, 1)
                dve.wait_ge(coef_ready, m + 1)

            def modulate(m, b, target):
                dve.wait_ge(turn_full[b % 2], 2 * m + b // 2 + 1)
                wait_used(dve, h_lo_done, GB * m + b - 1)
                for k in range(KD):
                    last = dve.tensor_scalar(target[:, k, :], turn[b % 2][:, k, :], coef[:, k, b:b + 1],
                                             coef[:, KD + k, b:b + 1], ALU.mult, ALU.add)
                last.then_inc(turn_read[b % 2], 1)

            def h_low(m, p, b, source):
                dve.wait_ge(h_hi_done, GB * m + b + 1)
                dve.tensor_tensor(h_lo[p][:, :, tokens(b)], source, h_hi[p][:, :, tokens(b)].bitcast(F32),
                                  ALU.subtract).then_inc(h_lo_done, 1)

            def h_attn(b):
                return h[:, :, tokens(b)]

            def h_of_next(n, b):
                return h_mlp[b % 2][:] if isinstance(n, int) and n == GROUPS - 1 else h_attn(b)

            def low_part(w, hi, lo, c):
                dve.wait_ge(prod_hi[c], w + 1)
                dve.tensor_tensor(lo[:, c, :], ring[c][:], hi[:, c, :].bitcast(F32),
                                  ALU.subtract).then_inc(prod_lo[c], 1)

            def film_coefs(f, film, bias, norm_w):
                dve.wait_ge(film_full, f + 1)
                for k in range(KD):
                    dve.tensor_scalar(film[:, k, :], film_ps[:, k, :], one_plus[:, f, k:k + 1],
                                      col(norm_w)[:, k:k + 1], ALU.add, ALU.mult).then_inc(film_read, 1)
                    dve.tensor_scalar(film[:, KD + k, :], film_ps[:, KD + k, :], col(bias)[:, KD + k:KD + k + 1],
                                      None, ALU.add).then_inc(film_read, 1)

            def setup():
                dve.wait_ge(loaded["vecs"], 16)
                for k in range(KD):
                    last = dve.tensor_copy(bv_wide[:, k, :], col("bv")[:, k:k + 1].broadcast_to([P, P]))
                last.then_inc(bv_wide_done, 1)
                dve.tensor_tensor_reduce(bq_bk_terms[:], col("bq"), col("bk"), 1.0, 0.0, ALU.mult, ALU.add,
                                         bq_bk[:]).then_inc(bq_bk_done, 1)
                for f, b in enumerate(("f1b", "f2b")):
                    dve.tensor_scalar(one_plus[:, f, :], col(b)[:, 0:KD], 1.0, None, ALU.add).then_inc(one_plus_done, 1)
                for c in range(KD):
                    low_part(0, qk_hi, qk_lo, c)
                normalize(0, 0, 0)
                normalize(0, 0, 1)
                dve.wait_ge(one_plus_done, 2)
                film_coefs(0, film1, "f1b", "n1")
                dve.wait_ge(film_read, 2 * KD)
                take_coef(0, film1, 0)
                dve.wait_ge(vec_full, 1)
                dve.tensor_copy(wk_bq[:], vec[:, 0:KD]).then_inc(vec_read, 1)
                dve.tensor_copy(wq_bk[:], vec[:, KD:2 * KD]).then_inc(vec_read, 1)
                modulate(0, 0, h_attn(0))
                normalize(0, 0, 2)
                modulate(0, 1, h_attn(1))
                normalize(0, 0, 3)
                h_low(0, 0, 0, h_attn(0))
                h_low(0, 0, 1, h_attn(1))
                low_part(1, vp_hi, vp_lo, 0)
                low_part(1, vp_hi, vp_lo, 1)
                modulate(0, 2, h_attn(2))
                modulate(0, 3, h_attn(3))
                h_low(0, 0, 2, h_attn(2))
                h_low(0, 0, 3, h_attn(3))
                low_part(1, vp_hi, vp_lo, 2)
                low_part(1, vp_hi, vp_lo, 3)
                dve.wait_ge(vec_read, 2)
                dve.wait_ge(bq_bk_done, 1)
                key_terms(0)
                dve.wait_ge(row_full, 1)
                dve.wait_ge(loaded["bp"], 16)
                dve.tensor_tensor(attn_bias[:], vec, bp_wide[:], ALU.add).then_inc(row_read, 1)
                film_coefs(1, film2, "f2b", "n2")

            def key_terms(m):
                dve.wait_ge(turn_read[1], 2 * m + 2)
                dve.tensor_scalar(key_bias[:], h[:, 0, :], wq_bk[:, 0:1], bq_bk[:], ALU.mult,
                                  ALU.add).then_inc(key_bias_done, 1)
                for k in range(1, KD):
                    dve.wait_ge(key_bias_done, KD * m + k)
                    dve.scalar_tensor_tensor(key_bias[:], h[:, k, :], wq_bk[:, k:k + 1], key_bias[:],
                                             ALU.mult, ALU.add).then_inc(key_bias_done, 1)

            def v_low(n, b):
                dve.wait_ge(v_hi_done, GB * n + b + 1)
                dve.tensor_tensor(v_lo[:, b, :], ring[b][:], v_hi[:, b, :].bitcast(F32),
                                  ALU.subtract).then_inc(ring_read[b], 1)

            def attention(n, p, i):
                q = 1 - p
                to_mlp = isinstance(n, int) and n == GROUPS - 1
                normalize(n + 1, q, 0)
                normalize(n + 1, q, 1)
                v_low(n, 0)
                dve.wait_ge(scored, n + 1)
                dve.tensor_reduce(top[:], score[:], AX_X, ALU.max).then_inc(top_done, 1)
                dve.wait_ge(top_done, n + 1)
                dve.tensor_scalar(exp_bias[:], top[:], -SCALE, None, ALU.mult).then_inc(bias_done, 1)
                if to_mlp:
                    take_coef(GROUPS, film2, 0)
                else:
                    take_coef(n + 1, film1, n + 1)
                v_low(n, 1)
                modulate(n + 1, 0, h_of_next(n, 0))
                normalize(n + 1, q, 2)
                modulate(n + 1, 1, h_of_next(n, 1))
                normalize(n + 1, q, 3)
                h_low(n + 1, q, 0, h_of_next(n, 0))
                h_low(n + 1, q, 1, h_of_next(n, 1))
                v_low(n, 2)
                dve.wait_ge(exp_done, GB * n + GB)
                dve.reciprocal(rden[:], den[:]).then_inc(rden_done, 1)
                modulate(n + 1, 2, h_of_next(n, 2))
                dve.wait_ge(pT_hi_done, n + 1)
                dve.tensor_tensor(pT_lo[:], pT[:], pT_hi[:].bitcast(F32), ALU.subtract).then_inc(pT_read, 1)
                modulate(n + 1, 3, h_of_next(n, 3))
                h_low(n + 1, q, 2, h_of_next(n, 2))
                h_low(n + 1, q, 3, h_of_next(n, 3))
                v_low(n, 3)
                dve.wait_ge(rden_done, n + 1)
                dve.wait_ge(biased, n + 1)
                for b in range(GB):
                    dve.wait_ge(ring_full[b], 3 * n + 3)
                    dve.scalar_tensor_tensor(x_in[p][:, b, :], ring[b][:], rden[:, b:b + 1], x_in[p][:, b, :],
                                             ALU.mult, ALU.add).then_inc(ring_read[b], 1)
                if not to_mlp:
                    key_terms(n + 1)

            def mlp(n, p, i):
                m, q = GROUPS + n + 1, 1 - p
                last = isinstance(n, int) and n == GROUPS - 1
                for j in range(KH):
                    r, use = j % 2, KH // 2 * n + j // 2
                    dve.wait_ge(hidden_read[r], use + 1)
                    dve.tensor_tensor(act_lo[r][:], act_full[r][:], act_hi[r][:].bitcast(F32),
                                      ALU.subtract).then_inc(act_lo_done[r], 1)
                    if last:
                        continue
                    if j == TURN_AT[0] - 1:
                        normalize(m, q, 0)
                        normalize(m, q, 1)
                        take_coef(m, film2, n + 1)
                    if j - 1 in TURN_AT:
                        b = TURN_AT.index(j - 1)
                        modulate(m, b, h_mlp[b % 2][:])
                        if b + 2 < GB:
                            normalize(m, q, b + 2)
                    if j - 2 in TURN_AT:
                        b = TURN_AT.index(j - 2)
                        h_low(m, q, b, h_mlp[b % 2][:])
                dve.wait_ge(biased, GROUPS + n + 1)
                for b in range(GB):
                    dve.wait_ge(total_full[b], n + 1)
                    dve.tensor_tensor(x_in[p][:, b, :], ring[b][:], x_in[p][:, b, :], ALU.add).then_inc(total_read[b], 1)

            setup()
            group_pairs(dve, PAIRS, attention)
            group_pairs(dve, PAIRS, mlp)


def kernel(**inputs):
    import numpy as np
    import concourse.bacc as bacc
    from concourse.bass_utils import run_bass_kernel_spmd

    def get(name):
        return np.asarray(inputs["L0_cond_" + name])

    def columns(v):
        return v.reshape(-1, P).T

    packed = np.concatenate([columns(get(n)) for n in (
        "norm1_w", "film1_b", "q_b", "k_b", "v_b", "norm2_w", "film2_b", "mlp_b1")], axis=1)
    arrays = {
        "x": np.asarray(inputs["x"]),
        "cols": packed,
        "rows": np.stack([get("proj_b"), get("mlp_b2")]),
        "condT": np.asarray(inputs["cond_1024"]).T,
        "wqT": get("q_w").T, "wkT": get("k_w").T, "wvT": get("v_w").T, "wp": get("proj_w"),
        "f1w": get("film1_w"), "f2w": get("film2_w"), "w1": get("mlp_w1"), "w2": get("mlp_w2"),
    }
    arrays = {f"{k}_dram": np.ascontiguousarray(v) for k, v in arrays.items()}
    nc = bacc.Bacc("TRN2", target_bir_lowering=False, num_devices=1)
    args = [nc.dram_tensor(k, v.shape, mybir.dt.from_np(v.dtype), kind="ExternalInput").ap()
            for k, v in arrays.items()]
    shape = arrays["x_dram"].shape
    out = nc.dram_tensor("out_dram", shape, F32, kind="ExternalOutput").ap()
    x2 = nc.dram_tensor("x2_scratch", shape, F32, kind="Internal").ap()
    cond_block_kernel(nc, *args, out, x2)
    result = run_bass_kernel_spmd(nc, [arrays], core_ids=[0])
    return result.results[0]["out_dram"]
```

```python
from contextlib import ExitStack

import concourse.bass as bass
from concourse import mybir

F32 = mybir.dt.float32
F32R = mybir.dt.float32r
ACT = mybir.ActivationFunctionType
ALU = mybir.AluOpType
AX_X = mybir.AxisListType.X

P = 128
EPS = 1e-6
GB = 4
TOK = GB * P
STAGE = 2
BLK = 32


def column_map(KD, KH):
    at, out = 0, {}
    for name, n in (("n1", KD), ("f1b", 2 * KD), ("bq", KD), ("bk", KD), ("bv", KD),
                    ("n2", KD), ("f2b", 2 * KD), ("b1", KH)):
        out[name] = (at, at + n)
        at += n
    return out


def split3(hi_a, lo_a, hi_b, lo_b):
    return ((hi_a, hi_b), (hi_a, lo_b), (lo_a, hi_b))


def wait_used(engine, sem, uses):
    if not isinstance(uses, int) or uses > 0:
        engine.wait_ge(sem, uses)


def group_pairs(engine, pairs, body):
    for p in range(2):
        body(p, p, 0)
    with engine.Fori(1, pairs - 1) as i:
        for p in range(2):
            body(2 * i + p, p, i)
    for p in range(2):
        body(2 * (pairs - 1) + p, p, pairs - 1)


def cond_block_kernel(nc, x, xT, cols, rows, condT, wqT, wkT, wq, wk, wvT, wp, f1w, f2w, w1, w2, out, x2):
    B, N, D = x.shape
    H = w1.shape[1]
    KD, KH = D // P, H // P
    GROUPS = B // GB
    PAIRS = GROUPS // 2
    SCALE = float(D) ** -0.5
    assert N == P and KD == GB and D == TOK and KH % 4 == 0
    cmap = column_map(KD, KH)

    with ExitStack() as ctx:
        def tensor(stack, name, shape, dt=F32):
            return stack.enter_context(nc.sbuf_tensor(name, shape, dt))

        def sem(name):
            return ctx.enter_context(nc.semaphore(name))

        def sems(name, n):
            return [sem(f"{name}{i}") for i in range(n)]

        def keep(name, shape, dt=F32):
            return tensor(ctx, name, shape, dt)

        vecs = keep("vecs", [P, cols.shape[1]])
        ident = keep("ident", [P, P])
        minus_half, eps_sum = keep("minus_half", [P, 1]), keep("eps_sum", [P, 1])
        b2_wide = keep("b2_wide", [P, D])
        film2 = keep("film2", [P, 2 * KD, B])
        x_in = [keep(f"x_in{p}", [P, GB, D]) for p in range(2)]
        sumsq, rstd = keep("sumsq", [P, GB]), keep("rstd", [P, GB])
        rstd_hi, rstd_lo = keep("rstd_hi", [P, GB], F32R), keep("rstd_lo", [P, GB], F32R)
        ones_r = keep("ones_r", [P, P], F32R)
        coef = keep("coef", [P, 2 * KD, GB])
        h_hi = [keep(f"h_hi{p}", [P, KD, TOK], F32R) for p in range(2)]
        h_lo = [keep(f"h_lo{p}", [P, KD, TOK], F32R) for p in range(2)]
        with ExitStack() as early:
            xT_in = tensor(early, "xT_in", [P, KD, TOK])
        with ExitStack() as early:
            x_norm = [tensor(early, f"x_norm{r}", [P, D]) for r in range(2)]
            h_mlp = [tensor(early, f"h_mlp{r}", [P, KD, P]) for r in range(2)]
        x_row = keep("x_row", [P, D])
        blocks = keep("blocks", [P, D // BLK, 2, BLK])
        h_half = keep("h_half", [P, P // BLK, KD, 2, BLK])
        stage = [keep(f"stage{r}", [P, D]) for r in range(STAGE)]

        with ExitStack() as early:
            wqT_sb, wkT_sb, wvT_sb, wp_sb = (tensor(early, n, [P, KD, D]) for n in ("wqT", "wkT", "wvT", "wp"))
            f1w_sb, f2w_sb = (tensor(early, n, [P, KD, 2 * D]) for n in ("f1w", "f2w"))
        with ExitStack() as early:
            wqT_lo, wkT_lo, wvT_lo, wp_lo = (tensor(early, n, [P, KD, D], F32R)
                                             for n in ("wqT_lo", "wkT_lo", "wvT_lo", "wp_lo"))
        w1_hi, w1_lo = keep("w1_hi", [P, KD, H], F32R), keep("w1_lo", [P, KD, H], F32R)

        with ExitStack() as attn:
            def own(name, shape, dt=F32):
                return tensor(attn, name, shape, dt)

            qk_hi, qk_lo, vp_hi, vp_lo = (own(n, [P, KD, D], F32R) for n in ("qk_hi", "qk_lo", "vp_hi", "vp_lo"))
            film1 = own("film1", [P, 2 * KD, B])
            attn_bias = own("attn_bias", [P, D])
            wk_bq, wq_bk, bq_bk_terms = (own(n, [P, KD]) for n in ("wk_bq", "wq_bk", "bq_bk_terms"))
            bq_bk = own("bq_bk", [P, 1])
            h = own("h", [P, KD, TOK])
            key_bias = own("key_bias", [P, TOK])
            v_hi, v_lo = own("v_hi", [P, GB, D], F32R), own("v_lo", [P, GB, D], F32R)
            probs = own("probs", [P, GB, P])
            top, exp_bias, den, rden = (own(n, [P, GB]) for n in ("top", "exp_bias", "den", "rden"))
            pT_hi, pT_lo = own("pT_hi", [P, TOK], F32R), own("pT_lo", [P, TOK], F32R)
            with ExitStack() as early:
                condT_sb = tensor(early, "condT", [P, KD, B])
                bv_hi, bv_lo = (tensor(early, n, [P, KD, P], F32R) for n in ("bv_hi", "bv_lo"))
                bp_wide = tensor(early, "bp_wide", [P, D])
                one_plus = tensor(early, "one_plus", [P, 2, KD])
            g = own("g", [P, KD, TOK])
        w2_hi, w2_lo = keep("w2_hi", [P, KH, D], F32R), keep("w2_lo", [P, KH, D], F32R)
        act_full = [keep(f"act_full{r}", [P, TOK]) for r in range(2)]
        act_hi = [keep(f"act_hi{r}", [P, TOK], F32R) for r in range(2)]
        act_lo = [keep(f"act_lo{r}", [P, TOK], F32R) for r in range(2)]

        def bank(name, shape):
            return ctx.enter_context(nc.psum_tensor(name, shape, F32))

        ring = [bank(f"ring{r}", [P, D]) for r in range(4)]
        turn = [bank(f"turn{r}", [P, KD, P]) for r in range(2)]
        score = bank("score", [P, GB, P])
        pT = bank("pT", [P, TOK])
        vec = score[:].rearrange("p b t -> p (b t)")
        film_ps = pT[:].rearrange("p (j b) -> p j b", j=2 * KD)
        hidden = [vec, pT[:]]

        loads = ("vecs", "condT", "f1w_shift", "f2w", "bp", "b2", "bq_row", "bk_row")
        loaded = {n: sem("loaded_" + n) for n in loads}
        qk_loaded = sems("qk_loaded", KD)
        f1w_loaded = sems("f1w_loaded", KD)
        wq_loaded, wk_loaded = sem("wq_loaded"), sem("wk_loaded")
        ident_zero, ident_done, const_done, bv_hi_done, bv_lo_done = (
            sem(n) for n in ("ident_zero", "ident_done", "const_done", "bv_hi_done", "bv_lo_done"))
        prod_full, prod_hi, prod_lo = (sems(n, KD) for n in ("prod_full", "prod_hi", "prod_lo"))
        vec_done, row_full, row_read = (sem(n) for n in ("vec_done", "row_full", "row_read"))
        film_full, film_read, one_plus_done, bq_bk_done = (
            sem(n) for n in ("film_full", "film_read", "one_plus_done", "bq_bk_done"))
        wv_loaded = sems("wv_loaded", KD)
        weights_hi, weights_lo = sem("weights_hi"), sem("weights_lo")
        ones_r_done = sem("ones_r_done")
        xT_loaded, rstd_hi_done, rstd_lo_done, diag_done, spread, x_scaled, h_done = (
            sem(n) for n in ("xT_loaded", "rstd_hi_done", "rstd_lo_done", "diag_done", "spread", "x_scaled", "h_done"))
        h_last_done = sem("h_last_done")
        x_loaded, stored = ([sems(f"{n}{p}_", GB) for p in range(2)] for n in ("x_loaded", "stored"))
        summed, eps_added, rstd_done, normed, biased = (
            sem(n) for n in ("summed", "eps_added", "rstd_done", "normed", "biased"))
        turn_full, modulated = sems("turn_full", 2), sems("modulated", 2)
        transposed, moved = sem("transposed"), sem("moved")
        coef_ready, h_hi_done, h_lo_done = sem("coef_ready"), sem("h_hi_done"), sem("h_lo_done")
        ring_full, ring_read = sems("ring_full", 4), sems("ring_read", 4)
        key_bias_done, v_hi_done, scored, top_done, bias_done, exp_done = (
            sem(n) for n in ("key_bias_done", "v_hi_done", "scored", "top_done", "bias_done", "exp_done"))
        pT_full, pT_hi_done, pT_read, rden_done = (sem(n) for n in ("pT_full", "pT_hi_done", "pT_read", "rden_done"))
        piece_loaded, piece_hi, pieces_split = sems("piece_loaded", STAGE), sem("piece_hi"), sem("pieces_split")
        hidden_full, hidden_read = sems("hidden_full", 2), sems("hidden_read", 2)
        act_hi_done, act_lo_done, act_used = sems("act_hi_done", 2), sems("act_lo_done", 2), sems("act_used", 2)
        total_full, total_read = sems("total_full", GB), sems("total_read", GB)

        xT_chunks = xT.rearrange("(k p) n -> p k n", p=P)
        x_groups, x2_groups, out_groups = (a.rearrange("(g b) t d -> g t b d", b=GB) for a in (x, x2, out))

        def col(name):
            a, b = cmap[name]
            return vecs[:, a:b]

        def tokens(b):
            return slice(b * P, (b + 1) * P)

        wqT_hi, wkT_hi, wvT_hi, wp_hi = h_hi[1], h_lo[1], v_hi, v_lo
        wq_sb, wk_sb, bk_row, bq_row = wqT_sb, wkT_sb, stage[0], stage[1]
        diag_hi, diag_lo = pT_hi, pT_lo
        square = turn[1][:].rearrange("p k t -> p (k t)")

        def before_mlp(n):
            return isinstance(n, int) and n == GROUPS - 1

        def piece(w_1, w_2, t):
            if t < KH:
                return w_1[:, :, t * P:(t + 1) * P]
            return w_2[:, t - KH, :].rearrange("p (a n) -> p a n", a=KD)

        def pool_low(n):
            return () if w1_pieces(n) else range(KD // 2)

        def stage_of(t):
            return stage[t % STAGE][:].rearrange("p (a n) -> p a n", a=KD)

        W1_AT = {n: range(c * KH // 4, (c + 1) * KH // 4) for c, n in enumerate((0, 1, GROUPS - 2, GROUPS - 1))}

        def w1_pieces(n):
            return W1_AT.get(n, ()) if isinstance(n, int) else ()

        SUM_AT, NORM_AT, FILM_AT, SPLIT_AT = 3, (4, 9), (8, 13), (9, 14)
        MOVES = (P // BLK) ** 2

        def h_mlp_of(n, b):
            if isinstance(n, int) and n == 0:
                return h_mlp[b % 2][:].rearrange("p k (t s) -> p k t s", s=BLK)
            return h_half[:, :, :, b % 2, :].rearrange("p t k s -> p k t s")

        def h_part(part, b):
            return part[:, :, tokens(b)].rearrange("p k (t s) -> p k t s", s=BLK)

        block = ctx.enter_context(nc.Block())

        @block.sync
        def _(sp):
            def chunked(a):
                return a.rearrange("(k p) n -> p k n", p=P)

            def load(m, use_source, p, b):
                sp.dma_start(x_in[p][:, b, :], use_source[m][:, b, :]).then_inc(x_loaded[p][b], 16)

            def load_xT(n):
                sp.dma_start(xT_in[:], xT_chunks[:, :, bass.ds(TOK * n, TOK)]).then_inc(xT_loaded, 16)

            def load_piece(t):
                if t >= STAGE:
                    sp.wait_ge(pieces_split, t - STAGE + 1)
                if t < KH:
                    src = w1[:, t * P:(t + 1) * P].rearrange("(k p) n -> p k n", p=P)
                else:
                    src = w2[(t - KH) * P:(t - KH + 1) * P, :].rearrange("p (a n) -> p a n", a=KD)
                sp.dma_start(stage_of(t), src).then_inc(piece_loaded[t % STAGE], 16)

            sp.dma_start(condT_sb[:], chunked(condT)).then_inc(loaded["condT"], 16)
            for j in range(KD):
                sp.dma_start(f1w_sb[:, :, tokens(j)], chunked(f1w)[:, :, tokens(j)]).then_inc(f1w_loaded[j], 16)
            for k in range(KD):
                sp.dma_start(wqT_sb[:, k, :], wqT[tokens(k), :]).then_inc(qk_loaded[k], 16)
                sp.dma_start(wkT_sb[:, k, :], wkT[tokens(k), :]).then_inc(qk_loaded[k], 16)
            sp.dma_start(vecs[:], cols).then_inc(loaded["vecs"], 16)
            sp.dma_start(f1w_sb[:, :, D:2 * D], chunked(f1w)[:, :, D:2 * D]).then_inc(loaded["f1w_shift"], 16)
            for k in range(KD):
                sp.dma_start(wvT_sb[:, k, :], wvT[tokens(k), :]).then_inc(wv_loaded[k], 16)
                sp.dma_start(wp_sb[:, k, :], wp[tokens(k), :]).then_inc(wv_loaded[k], 16)
            for b in range(GB):
                load(0, x_groups, 0, b)
            load_xT(0)
            for row, dst, name in ((0, bp_wide, "bp"), (1, b2_wide, "b2"), (2, bq_row, "bq_row"), (3, bk_row, "bk_row")):
                sp.dma_start(dst[:], rows[row:row + 1, :].broadcast_to([P, D])).then_inc(loaded[name], 16)
            sp.dma_start(f2w_sb[:], chunked(f2w)).then_inc(loaded["f2w"], 16)
            sp.wait_ge(prod_full[KD - 1], 1)
            sp.dma_start(wk_sb[:], chunked(wk)).then_inc(wk_loaded, 16)
            sp.dma_start(wq_sb[:], chunked(wq)).then_inc(wq_loaded, 16)
            for b in range(GB):
                load(1, x_groups, 1, b)
            sp.wait_ge(vec_done, 2 * KD)

            def attention(n, p, i):
                if not before_mlp(n):
                    sp.wait_ge(h_hi_done, GB * n + GB)
                    load_xT(n + 1)
                for t in w1_pieces(n):
                    load_piece(t)
                if isinstance(i, int) and n == GROUPS - 1:
                    for t in range(KH, KH + STAGE):
                        load_piece(t)
                for b in range(GB):
                    sp.wait_ge(ring_read[b], 3 * n + 3)
                    sp.dma_start(x2_groups[n][:, b, :], x_in[p][:, b, :]).then_inc(stored[p][b], 16)
                if isinstance(i, int) and n == GROUPS - 1:
                    for t in range(KH + STAGE, KH + 2 * STAGE):
                        load_piece(t)
                for b in range(GB):
                    sp.wait_ge(stored[p][b], 16 * i + 16)
                    if isinstance(i, int) and i == PAIRS - 1:
                        load(p, x2_groups, p, b)
                    else:
                        load(n + 2, x_groups, p, b)

            def move_half(n, half):
                sp.wait_ge(transposed, GB * n - GB + 2 * half + 2)
                for a in range(P // BLK):
                    for t in range(P // BLK):
                        sp.dma_start(h_half[a * BLK:(a + 1) * BLK, t],
                                     blocks[t * BLK:(t + 1) * BLK, a * KD:(a + 1) * KD]).then_inc(moved, 16)

            def mlp(n, p, i):
                first, last = (isinstance(n, int) and n == m for m in (0, GROUPS - 1))
                if first:
                    for t in range(KH + 2 * STAGE, 2 * KH):
                        if t == KH + 10:
                            move_half(n + 1, 0)
                        load_piece(t)
                elif not last:
                    move_half(n + 1, 0)
                if not last:
                    move_half(n + 1, 1)
                for b in range(GB):
                    sp.wait_ge(total_read[b], n + 1)
                    sp.dma_start(out_groups[n][:, b, :], x_in[p][:, b, :]).then_inc(stored[p][b], 16)
                if isinstance(i, int) and i == PAIRS - 1 and p == 0:
                    return
                for b in range(GB):
                    sp.wait_ge(stored[p][b], 16 * (PAIRS + i) + 16)
                    if not (isinstance(i, int) and i == PAIRS - 1):
                        load(n + 2, x2_groups, p, b)
                if isinstance(i, int) and i == PAIRS - 1:
                    for b in range(GB):
                        sp.wait_ge(stored[0][b], 16 * 2 * PAIRS)

            group_pairs(sp, PAIRS, attention)
            group_pairs(sp, PAIRS, mlp)

        @block.gpsimd
        def _(pool):
            nc.gpsimd.memset(ident[:], 0.0).then_inc(ident_zero, 1)
            pool.wait_ge(ident_zero, 1)
            nc.gpsimd.affine_select(out=ident[:], in_=ident[:], compare_op=ALU.not_equal, fill=1.0,
                                    base=0, pattern=[[-1, P]], channel_multiplier=1).then_inc(ident_done, 1)
            nc.gpsimd.memset(probs[:, 0, :], 1.0).then_inc(const_done, 1)
            nc.gpsimd.memset(minus_half[:], -0.5).then_inc(const_done, 1)
            nc.gpsimd.memset(eps_sum[:], EPS * D).then_inc(const_done, 1)
            pool.wait_ge(const_done, 3)
            nc.gpsimd.tensor_copy(ones_r[:], probs[:, 0, :]).then_inc(ones_r_done, 1)
            pool.wait_ge(ident_done, 1)
            pool.wait_ge(ones_r_done, 1)

            def norm(m):
                pool.wait_ge(summed, GB * m + GB)
                nc.gpsimd.tensor_tensor(rstd[:], sumsq[:], eps_sum[:].broadcast_to([P, GB]),
                                        ALU.add).then_inc(eps_added, 1)
                pool.wait_ge(eps_added, m + 1)
                nc.gpsimd.tensor_tensor(rstd[:], rstd[:], minus_half[:].broadcast_to([P, GB]),
                                        ALU.pow).then_inc(rstd_done, 1)

            def diagonals(m):
                pool.wait_ge(rstd_done, m + 1)
                nc.gpsimd.tensor_tensor(rstd_hi[:], rstd[:], ones_r[:, 0:GB].bitcast(F32),
                                        ALU.mult).then_inc(rstd_hi_done, 1)
                pool.wait_ge(rstd_hi_done, m + 1)
                nc.gpsimd.tensor_tensor(rstd_lo[:], rstd[:], rstd_hi[:].bitcast(F32),
                                        ALU.subtract).then_inc(rstd_lo_done, 1)
                for part, diag in ((rstd_hi, diag_hi), (rstd_lo, diag_lo)):
                    if part is rstd_lo:
                        pool.wait_ge(rstd_lo_done, m + 1)
                    nc.gpsimd.tensor_tensor(
                        diag[:].rearrange("p (b t) -> p b t", b=GB), ident[:].unsqueeze(1).broadcast_to([P, GB, P]),
                        part[:].bitcast(F32).unsqueeze(2).broadcast_to([P, GB, P]), ALU.mult).then_inc(diag_done, 1)

            def add_bias(p, row):
                for b in range(GB):
                    last = nc.gpsimd.tensor_tensor(x_in[p][:, b, :], x_in[p][:, b, :], row[:], ALU.add)
                last.then_inc(biased, 1)

            def split_piece(t):
                pool.wait_ge(piece_loaded[t % STAGE], 16 * (t // STAGE) + 16)
                nc.gpsimd.tensor_copy(piece(w1_hi, w2_hi, t), stage_of(t)).then_inc(piece_hi, 1)
                pool.wait_ge(piece_hi, t + 1)
                nc.gpsimd.tensor_tensor(piece(w1_lo, w2_lo, t), stage_of(t), piece(w1_hi, w2_hi, t).bitcast(F32),
                                        ALU.subtract).then_inc(pieces_split, 1)

            def h_low(m, p, k):
                pool.wait_ge(h_hi_done, KD * m + k + 1)
                nc.gpsimd.tensor_tensor(h_lo[p][:, k, :], h[:, k, :], h_hi[p][:, k, :].bitcast(F32),
                                        ALU.subtract).then_inc(h_lo_done, 1)

            def attention(n, p, i):
                norm(n + 1)
                if not before_mlp(n):
                    diagonals(n + 1)
                for t in w1_pieces(n):
                    split_piece(t)
                if before_mlp(n):
                    pool.wait_ge(normed, GB)
                add_bias(1 - p, b2_wide if before_mlp(n) else attn_bias)
                if not before_mlp(n):
                    for k in pool_low(n):
                        h_low(n + 1, 1 - p, k)

            def mlp(n, p, i):
                late = []
                if isinstance(n, int) and n == 0:
                    for b in range(GB):
                        pool.wait_ge(ring_read[b], 3 * GROUPS)
                    for t in range(KH, KH + KH // 2):
                        split_piece(t)
                    late = range(KH + KH // 2, 2 * KH)
                if not (isinstance(n, int) and n == GROUPS - 1):
                    norm(GROUPS + n + 1)
                    for t in late:
                        split_piece(t)
                    pool.wait_ge(normed, GB * (n + 1) + GB)
                    add_bias(1 - p, b2_wide)

            norm(0)
            diagonals(0)
            pool.wait_ge(row_read, 1)
            pool.wait_ge(loaded["b2"], 16)
            add_bias(0, attn_bias)
            pool.wait_ge(film_full, 2)
            pool.wait_ge(vec_done, 2 * KD)
            group_pairs(pool, PAIRS, attention)
            group_pairs(pool, PAIRS, mlp)

        @block.tensor
        def _(pe):
            def product(bank_ap, steps, full):
                for t, (a, b) in enumerate(steps):
                    mm = pe.matmul(bank_ap, a, b, start=t == 0, stop=t == len(steps) - 1)
                if full is not None:
                    mm.then_inc(full, 1)

            def spread_rstd(m):
                pe.wait_ge(diag_done, 2 * m + 2)
                wait_used(pe, x_scaled, KD * m)
                rows_ps = turn[0][:].rearrange("p k t -> p (k t)")
                pe.matmul(rows_ps, ones_r[:], diag_hi[:], start=True, stop=False)
                pe.matmul(rows_ps, ones_r[:], diag_lo[:], start=False, stop=True).then_inc(spread, 1)

            def transpose_x(b):
                r = b % 2
                pe.wait_ge(normed, b + 1)
                wait_used(pe, modulated[r], b // 2)
                for k in range(KD):
                    mm = pe.transpose(turn[r][:, k, :], x_norm[r][:, k * P:(k + 1) * P], ident[:])
                mm.then_inc(turn_full[r], 1)

            def film_product(w, j):
                product(film_ps[:, j, :], [(w[:, k, tokens(j)], condT_sb[:, k, :]) for k in range(KD)],
                        film_full if j == 2 * KD - 1 else None)

            def setup():
                def weight_product(w, k, a_hi, a_lo, b_hi, b_lo):
                    pe.wait_ge(weights_hi, 2 * (KD * w + k) + 2)
                    pe.wait_ge(weights_lo, 2 * (KD * w + k) + 2)
                    for c in range(KD):
                        if w == 1 and k == 0:
                            pe.wait_ge(prod_lo[c], 1)
                        for t, (a, b) in enumerate(split3(a_hi[:, k, tokens(c)], a_lo[:, k, tokens(c)],
                                                          b_hi[:, k, :], b_lo[:, k, :])):
                            mm = pe.matmul(ring[c][:], a, b, start=k == 0 and t == 0, stop=k == KD - 1 and t == 2)
                        if k == KD - 1:
                            mm.then_inc(prod_full[c], 1)

                pe.wait_ge(loaded["condT"], 16)
                for j in range(KD):
                    pe.wait_ge(f1w_loaded[j], 16)
                    film_product(f1w_sb, j)
                for k in range(KD):
                    weight_product(0, k, wqT_hi, wqT_lo, wkT_hi, wkT_lo)
                pe.wait_ge(loaded["f1w_shift"], 16)
                for j in range(KD, 2 * KD):
                    film_product(f1w_sb, j)
                for k in range(KD):
                    if k == KD - 1:
                        pe.wait_ge(ones_r_done, 1)
                        spread_rstd(0)
                    weight_product(1, k, wvT_hi, wvT_lo, wp_hi, wp_lo)
                pe.wait_ge(bv_hi_done, 1)
                pe.wait_ge(bv_lo_done, 1)
                product(vec, [t for k in range(KD) for t in split3(
                    bv_hi[:, k, :], bv_lo[:, k, :], wp_hi[:, k, :], wp_lo[:, k, :])], row_full)
                pe.wait_ge(loaded["f2w"], 16)
                pe.wait_ge(film_read, 2 * KD)
                for j in range(2 * KD):
                    film_product(f2w_sb, j)
                for c in range(KD):
                    pe.wait_ge(prod_lo[c], 2)

            def g_product(n, p):
                pe.wait_ge(h_hi_done, GB * n + GB)
                for j in range(KD):
                    wait_used(pe, ring_read[j], 3 * n)
                    for k in range(KD):
                        pe.matmul(ring[j][:], qk_hi[:, k, tokens(j)], h_hi[p][:, k, :], start=k == 0, stop=False)
                        pe.matmul(ring[j][:], qk_lo[:, k, tokens(j)], h_hi[p][:, k, :], start=False, stop=False)
                    pe.wait_ge(h_lo_done, GB * n + GB)
                    for k in range(KD):
                        mm = pe.matmul(ring[j][:], qk_hi[:, k, tokens(j)], h_lo[p][:, k, :],
                                       start=False, stop=k == KD - 1)
                    mm.then_inc(ring_full[j], 1)

            def v_product(n, p, b):
                pe.wait_ge(ring_read[b], 3 * n + 1)
                product(ring[b][:], [t for k in range(KD) for t in split3(
                    h_hi[p][:, k, tokens(b)], h_lo[p][:, k, tokens(b)], vp_hi[:, k, :], vp_lo[:, k, :])], ring_full[b])

            def scores(n):
                for j in range(KD):
                    pe.wait_ge(ring_read[j], 3 * n + 1)
                pe.wait_ge(key_bias_done, KD * n + KD)
                if isinstance(n, int) and n == 0:
                    pe.wait_ge(row_read, 1)
                    pe.wait_ge(ones_r_done, 1)
                wait_used(pe, exp_done, GB * n)
                for b in range(GB):
                    product(score[:, b, :],
                            [(g[:, k, tokens(b)], h[:, k, tokens(b)]) for k in range(KD)]
                            + [(key_bias[:, tokens(b)], ones_r[:].bitcast(F32))], scored if b == GB - 1 else None)

            def transpose_probs(n):
                pe.wait_ge(exp_done, GB * n + GB)
                if isinstance(n, int) and n == 0:
                    pe.wait_ge(film_read, 4 * KD)
                wait_used(pe, pT_read, n)
                for b in range(GB):
                    mm = pe.transpose(pT[:, tokens(b)], probs[:, b, :], ident[:])
                mm.then_inc(pT_full, 1)

            def output(n, b):
                pe.wait_ge(pT_read, n + 1)
                pe.wait_ge(ring_read[b], 3 * n + 2)
                product(ring[b][:], split3(pT_hi[:, tokens(b)], pT_lo[:, tokens(b)], v_hi[:, b, :], v_lo[:, b, :]),
                        ring_full[b])

            def attention(n, p, i):
                g_product(n, p)
                v_product(n, p, 0)
                scores(n)
                if not before_mlp(n):
                    spread_rstd(n + 1)
                v_product(n, p, 1)
                if before_mlp(n):
                    pe.wait_ge(x_scaled, KD * GROUPS)
                    transpose_x(0)
                    transpose_x(1)
                v_product(n, p, 2)
                if before_mlp(n):
                    transpose_x(2)
                    transpose_x(3)
                transpose_probs(n)
                v_product(n, p, 3)
                for b in range(GB):
                    output(n, b)

            def up(n, p, j):
                if j == 0:
                    pe.wait_ge(h_hi_done, GB * (GROUPS + n) + GB)
                    pe.wait_ge(h_lo_done, GB * (GROUPS + n) + GB)
                    if isinstance(n, int) and n == 0:
                        pe.wait_ge(exp_done, GB * GROUPS)
                        pe.wait_ge(pT_read, GROUPS)
                        pe.wait_ge(pieces_split, KH)
                wait_used(pe, hidden_read[j % 2], KH // 2 * n + j // 2)
                product(hidden[j % 2], [t for k in range(KD) for t in split3(
                    w1_hi[:, k, tokens(j)], w1_lo[:, k, tokens(j)], h_hi[p][:, k, :], h_lo[p][:, k, :])],
                    hidden_full[j % 2])

            def down(n, j):
                r, use = j % 2, KH // 2 * n + j // 2
                pe.wait_ge(act_hi_done[r], use + 1)
                if isinstance(n, int) and n == 0:
                    pe.wait_ge(pieces_split, KH + j + 1)
                if isinstance(n, int) and n == GROUPS - 1 and j == KH - 1:
                    pe.wait_ge(act_lo_done[r], use + 1)
                    for b in range(GB):
                        for t, (a, w) in enumerate(split3(act_hi[r][:, tokens(b)], act_lo[r][:, tokens(b)],
                                                          w2_hi[:, j, :], w2_lo[:, j, :])):
                            mm = pe.matmul(ring[b][:], a, w, start=False, stop=t == 2)
                        mm.then_inc(total_full[b], 1)
                    return
                for b in range(GB):
                    if j == 0:
                        wait_used(pe, total_read[b], n)
                    pe.matmul(ring[b][:], act_hi[r][:, tokens(b)], w2_hi[:, j, :], start=j == 0, stop=False)
                    pe.matmul(ring[b][:], act_hi[r][:, tokens(b)], w2_lo[:, j, :], start=False, stop=False)
                pe.wait_ge(act_lo_done[r], use + 1)
                for b in range(GB):
                    mm = pe.matmul(ring[b][:], act_lo[r][:, tokens(b)], w2_hi[:, j, :],
                                   start=False, stop=j == KH - 1)
                    if j == KH - 1:
                        mm.then_inc(total_full[b], 1)
                if j < KH - 1:
                    mm.then_inc(act_used[r], 1)

            def mlp(n, p, i):
                last = isinstance(n, int) and n == GROUPS - 1
                up(n, p, 0)
                for j in range(KH):
                    if j + 1 < KH:
                        up(n, p, j + 1)
                    down(n, j)

            setup()
            group_pairs(pe, PAIRS, attention)
            group_pairs(pe, PAIRS, mlp)

        @block.scalar
        def _(act):
            def sum_squares(m, p, use, b):
                act.wait_ge(x_loaded[p][b], 16 * use + 16)
                if b == 0:
                    wait_used(act, rstd_done, m)
                wait_used(act, summed, GB * m + b)
                nc.scalar.activation(square, x_in[p][:, b, :], ACT.Square,
                                     accum_out=sumsq[:, b:b + 1]).then_inc(summed, 1)

            def modulate_last(m):
                k = KD - 1
                act.wait_ge(x_scaled, KD * m + k + 1)
                act.wait_ge(coef_ready, m + 1)
                for b in range(GB):
                    last = nc.scalar.activation(h[:, k, tokens(b)], xT_in[:, k, tokens(b)], ACT.Identity,
                                                bias=coef[:, KD + k, b:b + 1], scale=coef[:, k, b:b + 1])
                last.then_inc(h_last_done, 1)

            def h_high(m, p, k):
                if k < KD - 1:
                    act.wait_ge(h_done, (KD - 1) * m + k + 1)
                else:
                    act.wait_ge(h_last_done, m + 1)
                nc.scalar.copy(h_hi[p][:, k, :], h[:, k, :]).then_inc(h_hi_done, 1)

            def h_high_mlp(n, p, b):
                act.wait_ge(modulated[b % 2], 2 * n + b // 2 + 1)
                nc.scalar.copy(h_part(h_hi[p], b), h_mlp_of(n, b)).then_inc(h_hi_done, 1)

            def modulate(n, b):
                act.wait_ge(coef_ready, GROUPS + n + 1)
                if isinstance(n, int) and n == 0:
                    act.wait_ge(turn_full[1], b // 2 + 1)
                    act.wait_ge(h_lo_done, GB * GROUPS + b - 1)
                    source = turn[1][:].rearrange("p k (t s) -> p k t s", s=BLK)
                else:
                    act.wait_ge(moved, 16 * MOVES * (2 * n - 2 + b // 2 + 1))
                    source = h_mlp_of(n, b)
                for k in range(KD):
                    last = nc.scalar.activation(h_mlp_of(n, b)[:, k], source[:, k], ACT.Identity,
                                                bias=coef[:, KD + k, b:b + 1], scale=coef[:, k, b:b + 1])
                last.then_inc(modulated[1], 1)

            def high_part(w, hi, c):
                act.wait_ge(prod_full[c], w + 1)
                nc.scalar.copy(hi[:, c, :], ring[c][:]).then_inc(prod_hi[c], 1)

            def v_high(n, b):
                act.wait_ge(ring_full[b], 3 * n + 2)
                nc.scalar.copy(v_hi[:, b, :], ring[b][:]).then_inc(v_hi_done, 1)

            def attention(n, p, i):
                for j in range(KD):
                    act.wait_ge(ring_full[j], 3 * n + 1)
                    nc.scalar.activation(g[:, j, :], ring[j][:], ACT.Identity,
                                         bias=wk_bq[:, j:j + 1]).then_inc(ring_read[j], 1)
                    if j >= 1:
                        sum_squares(n + 1, 1 - p, i + p, j - 1)
                sum_squares(n + 1, 1 - p, i + p, GB - 1)
                v_high(n, 0)
                act.wait_ge(bias_done, n + 1)
                for b in range(GB):
                    nc.scalar.activation(probs[:, b, :], score[:, b, :], ACT.Exp, bias=exp_bias[:, b:b + 1],
                                         scale=SCALE, accum_out=den[:, b:b + 1]).then_inc(exp_done, 1)
                v_high(n, 1)
                if before_mlp(n):
                    modulate(0, 1)
                    h_high_mlp(0, 1 - p, 0)
                    h_high_mlp(0, 1 - p, 1)
                    v_high(n, 2)
                    modulate(0, 3)
                else:
                    modulate_last(n + 1)
                    h_high(n + 1, 1 - p, 0)
                    h_high(n + 1, 1 - p, 1)
                    v_high(n, 2)
                act.wait_ge(pT_full, n + 1)
                nc.scalar.copy(pT_hi[:], pT[:]).then_inc(pT_hi_done, 1)
                if before_mlp(n):
                    h_high_mlp(0, 1 - p, 2)
                    v_high(n, 3)
                    h_high_mlp(0, 1 - p, 3)
                else:
                    h_high(n + 1, 1 - p, 2)
                    v_high(n, 3)
                    h_high(n + 1, 1 - p, 3)

            def gelu(n, j):
                r, use = j % 2, KH // 2 * n + j // 2
                act.wait_ge(hidden_full[r], use + 1)
                if r == 0:
                    wait_used(act, act_used[0], use)
                elif j == 1:
                    wait_used(act, total_full[GB - 1], n)
                else:
                    act.wait_ge(act_used[1], (KH // 2 - 1) * n + j // 2)
                b1 = col("b1")[:, j:j + 1]
                nc.scalar.activation(act_hi[r][:], hidden[r], ACT.Gelu, bias=b1).then_inc(act_hi_done[r], 1)
                nc.scalar.activation(act_full[r][:], hidden[r], ACT.Gelu, bias=b1).then_inc(hidden_read[r], 1)

            def mlp(n, p, i):
                last = isinstance(n, int) and n == GROUPS - 1
                if isinstance(n, int) and n == 0:
                    for b in range(GB):
                        act.wait_ge(ring_read[b], 3 * GROUPS)
                for j in range(KH):
                    gelu(n, j)
                    if not last and j == SUM_AT:
                        for b in range(GB):
                            sum_squares(GROUPS + n + 1, 1 - p, PAIRS + i + p, b)
                    if not last and j in FILM_AT:
                        modulate(n + 1, 2 * FILM_AT.index(j) + 1)
                    if not last and j in SPLIT_AT:
                        for b in range(2):
                            h_high_mlp(n + 1, 1 - p, 2 * SPLIT_AT.index(j) + b)

            for w, part_loaded, pairs in ((0, qk_loaded, ((wqT_hi, wqT_sb), (wkT_hi, wkT_sb))),
                                          (1, wv_loaded, ((wvT_hi, wvT_sb), (wp_hi, wp_sb)))):
                for k in range(KD):
                    act.wait_ge(part_loaded[k], 32)
                    for hi, src in pairs:
                        nc.scalar.copy(hi[:, k, :], src[:, k, :]).then_inc(weights_hi, 1)
            for c in range(KD):
                high_part(0, qk_hi, c)
            for b in range(GB):
                sum_squares(0, 0, 0, b)
            modulate_last(0)
            for k in range(KD):
                h_high(0, 0, k)
            for c in range(KD):
                high_part(1, vp_hi, c)
            act.wait_ge(vec_done, 2 * KD)
            act.wait_ge(row_read, 1)
            act.wait_ge(film_read, 4 * KD)
            group_pairs(act, PAIRS, attention)
            group_pairs(act, PAIRS, mlp)

        @block.vector
        def _(dve):
            def scale_x(m, k):
                if k == 0:
                    dve.wait_ge(xT_loaded, 16 * m + 16)
                    dve.wait_ge(spread, m + 1)
                dve.scalar_tensor_tensor(xT_in[:, k, :], xT_in[:, k, :], float(D) ** 0.5,
                                         turn[0][:].rearrange("p k t -> p (k t)"), ALU.mult,
                                         ALU.mult).then_inc(x_scaled, 1)

            def modulate_attn(m, k):
                dve.wait_ge(x_scaled, KD * m + k + 1)
                for b in range(GB):
                    last = dve.tensor_scalar(h[:, k, tokens(b)], xT_in[:, k, tokens(b)], coef[:, k, b:b + 1],
                                             coef[:, KD + k, b:b + 1], ALU.mult, ALU.add)
                last.then_inc(h_done, 1)

            def h_low_attn(m, p, k):
                dve.wait_ge(h_hi_done, KD * m + k + 1)
                dve.tensor_tensor(h_lo[p][:, k, :], h[:, k, :], h_hi[p][:, k, :].bitcast(F32),
                                  ALU.subtract).then_inc(h_lo_done, 1)

            def normalize(p, b):
                dve.wait_ge(rstd_done, GROUPS + 1)
                wait_used(dve, turn_full[b % 2], b // 2)
                dve.tensor_scalar(x_norm[b % 2][:].rearrange("p (k a s) -> p a k s", k=KD, s=BLK),
                                  x_in[p][:, b, :].rearrange("p (a k s) -> p a k s", k=KD, s=BLK),
                                  rstd[:, b:b + 1], float(D) ** 0.5, ALU.mult, ALU.mult).then_inc(normed, 1)

            def normalize_and_turn(n, p, b):
                dve.wait_ge(rstd_done, GROUPS + n + 1)
                wait_used(dve, transposed, GB * n - GB + b)
                dve.tensor_scalar(x_row[:], x_in[p][:, b, :], rstd[:, b:b + 1], float(D) ** 0.5,
                                  ALU.mult, ALU.mult).then_inc(normed, 1)
                dve.wait_ge(normed, GB * n + b + 1)
                wait_used(dve, moved, 16 * MOVES * (2 * n - 2 + b // 2))
                if b % 2 == 0:
                    dve.wait_ge(h_lo_done, GB * (GROUPS + n) + b)
                dve.transpose(blocks[:, :, b % 2, :],
                              x_row[:].rearrange("p (c s) -> p c s", s=BLK)).then_inc(transposed, 1)

            def take_coef(m, film, group):
                dve.tensor_copy(coef[:], film[:, :, bass.ds(GB * group, GB)]).then_inc(coef_ready, 1)
                dve.wait_ge(coef_ready, m + 1)

            def modulate(n, b):
                if isinstance(n, int) and n == 0:
                    dve.wait_ge(turn_full[0], b // 2 + 1)
                    dve.wait_ge(h_lo_done, GB * GROUPS + b - 1)
                    source = turn[0][:].rearrange("p k (t s) -> p k t s", s=BLK)
                else:
                    dve.wait_ge(moved, 16 * MOVES * (2 * n - 2 + b // 2 + 1))
                    source = h_mlp_of(n, b)
                for k in range(KD):
                    last = dve.tensor_scalar(h_mlp_of(n, b)[:, k], source[:, k], coef[:, k, b:b + 1],
                                             coef[:, KD + k, b:b + 1], ALU.mult, ALU.add)
                last.then_inc(modulated[0], 1)

            def h_low(n, p, b):
                dve.wait_ge(h_hi_done, GB * (GROUPS + n) + b + 1)
                dve.tensor_tensor(h_part(h_lo[p], b), h_mlp_of(n, b), h_part(h_hi[p][:].bitcast(F32), b),
                                  ALU.subtract).then_inc(h_lo_done, 1)

            def low_part(w, hi, lo, c):
                dve.wait_ge(prod_hi[c], w + 1)
                dve.tensor_tensor(lo[:, c, :], ring[c][:], hi[:, c, :].bitcast(F32),
                                  ALU.subtract).then_inc(prod_lo[c], 1)

            def film_coefs(f, film, bias, norm_w):
                dve.wait_ge(film_full, f + 1)
                for k in range(KD):
                    dve.tensor_scalar(film[:, k, :], film_ps[:, k, :], one_plus[:, f, k:k + 1],
                                      col(norm_w)[:, k:k + 1], ALU.add, ALU.mult).then_inc(film_read, 1)
                    dve.tensor_scalar(film[:, KD + k, :], film_ps[:, KD + k, :], col(bias)[:, KD + k:KD + k + 1],
                                      None, ALU.add).then_inc(film_read, 1)

            def weights_low(w, k, a_sb, a_hi, a_lo, b_sb, b_hi, b_lo):
                dve.wait_ge(weights_hi, 2 * (KD * w + k) + 2)
                for src, hi, lo in ((a_sb, a_hi, a_lo), (b_sb, b_hi, b_lo)):
                    dve.tensor_tensor(lo[:, k, :], src[:, k, :], hi[:, k, :].bitcast(F32),
                                      ALU.subtract).then_inc(weights_lo, 1)

            def row_sums(w_sb, row, into):
                for c in range(KD):
                    dve.tensor_tensor_reduce(w_sb[:, c, :], w_sb[:, c, :], row[:], 1.0, 0.0, ALU.mult, ALU.add,
                                             into[:, c:c + 1]).then_inc(vec_done, 1)

            def setup():
                for k in range(KD):
                    weights_low(0, k, wqT_sb, wqT_hi, wqT_lo, wkT_sb, wkT_hi, wkT_lo)
                dve.wait_ge(loaded["vecs"], 16)
                for k in range(KD):
                    last = dve.tensor_copy(bv_hi[:, k, :], col("bv")[:, k:k + 1].broadcast_to([P, P]))
                last.then_inc(bv_hi_done, 1)
                dve.tensor_tensor_reduce(bq_bk_terms[:], col("bq"), col("bk"), 1.0, 0.0, ALU.mult, ALU.add,
                                         bq_bk[:]).then_inc(bq_bk_done, 1)
                for f, b in enumerate(("f1b", "f2b")):
                    dve.tensor_scalar(one_plus[:, f, :], col(b)[:, 0:KD], 1.0, None, ALU.add).then_inc(one_plus_done, 1)
                dve.wait_ge(bv_hi_done, 1)
                for k in range(KD):
                    last = dve.tensor_tensor(bv_lo[:, k, :], col("bv")[:, k:k + 1].broadcast_to([P, P]),
                                             bv_hi[:, k, :].bitcast(F32), ALU.subtract)
                last.then_inc(bv_lo_done, 1)
                for k in range(KD):
                    weights_low(1, k, wvT_sb, wvT_hi, wvT_lo, wp_sb, wp_hi, wp_lo)
                for c in range(KD):
                    low_part(0, qk_hi, qk_lo, c)
                dve.wait_ge(one_plus_done, 2)
                film_coefs(0, film1, "f1b", "n1")
                dve.wait_ge(film_read, 2 * KD)
                take_coef(0, film1, 0)
                for k in range(KD):
                    scale_x(0, k)
                for k in range(KD - 1):
                    modulate_attn(0, k)
                for k in range(KD):
                    h_low_attn(0, 0, k)
                for c in range(KD):
                    low_part(1, vp_hi, vp_lo, c)
                dve.wait_ge(loaded["bq_row"], 16)
                dve.wait_ge(wk_loaded, 16)
                row_sums(wk_sb, bq_row, wk_bq)
                dve.wait_ge(row_full, 1)
                dve.wait_ge(loaded["bp"], 16)
                dve.tensor_tensor(attn_bias[:], vec, bp_wide[:], ALU.add).then_inc(row_read, 1)
                dve.wait_ge(loaded["bk_row"], 16)
                dve.wait_ge(wq_loaded, 16)
                row_sums(wq_sb, bk_row, wq_bk)
                film_coefs(1, film2, "f2b", "n2")
                dve.wait_ge(vec_done, 2 * KD)
                dve.wait_ge(bq_bk_done, 1)
                key_terms(0)

            def key_terms(m):
                dve.wait_ge(h_done, (KD - 1) * m + KD - 1)
                dve.wait_ge(h_last_done, m + 1)
                dve.tensor_scalar(key_bias[:], h[:, 0, :], wq_bk[:, 0:1], bq_bk[:], ALU.mult,
                                  ALU.add).then_inc(key_bias_done, 1)
                for k in range(1, KD):
                    dve.wait_ge(key_bias_done, KD * m + k)
                    dve.scalar_tensor_tensor(key_bias[:], h[:, k, :], wq_bk[:, k:k + 1], key_bias[:],
                                             ALU.mult, ALU.add).then_inc(key_bias_done, 1)

            def v_low(n, b):
                dve.wait_ge(v_hi_done, GB * n + b + 1)
                dve.tensor_tensor(v_lo[:, b, :], ring[b][:], v_hi[:, b, :].bitcast(F32),
                                  ALU.subtract).then_inc(ring_read[b], 1)

            def attention(n, p, i):
                q = 1 - p
                to_mlp = before_mlp(n)
                if to_mlp:
                    normalize(q, 0)
                    normalize(q, 1)
                v_low(n, 0)
                dve.wait_ge(scored, n + 1)
                dve.tensor_reduce(top[:], score[:], AX_X, ALU.max).then_inc(top_done, 1)
                dve.wait_ge(top_done, n + 1)
                dve.tensor_scalar(exp_bias[:], top[:], -SCALE, None, ALU.mult).then_inc(bias_done, 1)
                if to_mlp:
                    take_coef(GROUPS, film2, 0)
                else:
                    take_coef(n + 1, film1, n + 1)
                if to_mlp:
                    normalize(q, 2)
                    modulate(0, 0)
                    normalize(q, 3)
                    v_low(n, 1)
                    h_low(0, q, 0)
                else:
                    for k in range(KD):
                        scale_x(n + 1, k)
                    for k in range(KD - 1):
                        modulate_attn(n + 1, k)
                if to_mlp:
                    dve.wait_ge(exp_done, GB * n + GB)
                    dve.reciprocal(rden[:], den[:]).then_inc(rden_done, 1)
                    h_low(0, q, 1)
                    modulate(0, 2)
                dve.wait_ge(pT_hi_done, n + 1)
                dve.tensor_tensor(pT_lo[:], pT[:], pT_hi[:].bitcast(F32), ALU.subtract).then_inc(pT_read, 1)
                if not to_mlp:
                    v_low(n, 1)
                    dve.wait_ge(exp_done, GB * n + GB)
                    dve.reciprocal(rden[:], den[:]).then_inc(rden_done, 1)
                v_low(n, 2)
                if to_mlp:
                    h_low(0, q, 2)
                else:
                    if not pool_low(n):
                        h_low_attn(n + 1, q, 0)
                v_low(n, 3)
                dve.wait_ge(rden_done, n + 1)
                dve.wait_ge(biased, n + 1)
                for b in range(GB):
                    if b == 1:
                        if to_mlp:
                            h_low(0, q, 3)
                        else:
                            for k in range(1, KD):
                                if k not in pool_low(n):
                                    h_low_attn(n + 1, q, k)
                    dve.wait_ge(ring_full[b], 3 * n + 3)
                    dve.scalar_tensor_tensor(x_in[p][:, b, :], ring[b][:], rden[:, b:b + 1], x_in[p][:, b, :],
                                             ALU.mult, ALU.add).then_inc(ring_read[b], 1)
                if not to_mlp:
                    key_terms(n + 1)

            def mlp(n, p, i):
                q = 1 - p
                last = isinstance(n, int) and n == GROUPS - 1
                for j in range(KH):
                    r, use = j % 2, KH // 2 * n + j // 2
                    dve.wait_ge(hidden_read[r], use + 1)
                    dve.tensor_tensor(act_lo[r][:], act_full[r][:], act_hi[r][:].bitcast(F32),
                                      ALU.subtract).then_inc(act_lo_done[r], 1)
                    if last:
                        continue
                    if j in FILM_AT:
                        modulate(n + 1, 2 * FILM_AT.index(j))
                    if j in SPLIT_AT:
                        for b in range(2):
                            h_low(n + 1, q, 2 * SPLIT_AT.index(j) + b)
                    if j in NORM_AT:
                        for b in range(2):
                            normalize_and_turn(n + 1, q, 2 * NORM_AT.index(j) + b)
                    if j == NORM_AT[0]:
                        take_coef(GROUPS + n + 1, film2, n + 1)
                dve.wait_ge(biased, GROUPS + n + 1)
                for b in range(GB):
                    dve.wait_ge(total_full[b], n + 1)
                    dve.tensor_tensor(x_in[p][:, b, :], ring[b][:], x_in[p][:, b, :], ALU.add).then_inc(total_read[b], 1)

            setup()
            group_pairs(dve, PAIRS, attention)
            group_pairs(dve, PAIRS, mlp)


def kernel(**inputs):
    import numpy as np
    import concourse.bacc as bacc
    from concourse.bass_utils import run_bass_kernel_spmd

    def get(name):
        return np.asarray(inputs["L0_cond_" + name])

    def columns(v):
        return v.reshape(-1, P).T

    def by_blocks(a):
        n = P // BLK
        return a.reshape(*a.shape[:-1], -1, n, n, BLK).swapaxes(-3, -2).reshape(a.shape)

    packed = np.concatenate([columns(v) for v in (
        *(get(n) for n in ("norm1_w", "film1_b", "q_b", "k_b", "v_b")),
        by_blocks(get("norm2_w")), by_blocks(get("film2_b")), get("mlp_b1"))], axis=1)
    arrays = {
        "x": np.asarray(inputs["x"]),
        "xT": np.asarray(inputs["x"]).reshape(-1, inputs["x"].shape[-1]).T,
        "cols": packed,
        "rows": np.stack([get("proj_b"), get("mlp_b2"), get("q_b"), get("k_b")]),
        "condT": np.asarray(inputs["cond_1024"]).T,
        "wqT": get("q_w").T, "wkT": get("k_w").T, "wq": get("q_w"), "wk": get("k_w"), "wvT": get("v_w").T, "wp": get("proj_w"),
        "f1w": get("film1_w"), "f2w": by_blocks(get("film2_w")), "w1": by_blocks(get("mlp_w1").T).T, "w2": get("mlp_w2"),
    }
    arrays = {f"{k}_dram": np.ascontiguousarray(v) for k, v in arrays.items()}
    nc = bacc.Bacc("TRN2", target_bir_lowering=False, num_devices=1)
    args = [nc.dram_tensor(k, v.shape, mybir.dt.from_np(v.dtype), kind="ExternalInput").ap()
            for k, v in arrays.items()]
    shape = arrays["x_dram"].shape
    out = nc.dram_tensor("out_dram", shape, F32, kind="ExternalOutput").ap()
    x2 = nc.dram_tensor("x2_scratch", shape, F32, kind="Internal").ap()
    cond_block_kernel(nc, *args, out, x2)
    result = run_bass_kernel_spmd(nc, [arrays], core_ids=[0])
    return result.results[0]["out_dram"]
```
